# Optimizing a Trainium2 kernel written in Bass

```python
import numpy as np
import jax
import jax.numpy as jnp

def _softmax(x, axis=-1):
    return jax.nn.softmax(x, axis=axis)

def _gelu(x):
    return jax.nn.gelu(x, approximate=True)

def _silu(x):
    return jax.nn.silu(x)

def _sigmoid(x):
    return jax.nn.sigmoid(x)

def _layernorm(x, axis=-1, eps=1e-05):
    m = jnp.mean(x, axis=axis, keepdims=True)
    v = jnp.var(x, axis=axis, keepdims=True)
    return (x - m) / jnp.sqrt(v + eps)

def _scatter_add(tgt, idx, src, axis=0):
    return tgt.at[idx].add(src)

def _segment_sum(src, seg, n):
    return jax.ops.segment_sum(src, seg, n)
kernel_name = 'mk_sandwich_d1_jaxref_r8_140a74'

def setup_inputs(seed: int=0):
    np.random.seed(seed)
    _w = jnp.asarray

    def _L0_attn_setup():
        import jax, jax.numpy as jnp
        import numpy as np
        D_MODEL, N_HEADS, N_KV, HEAD_DIM, D_LAT = (128, 8, 2, 128, 32)
        N_REP = N_HEADS // N_KV
        B, T = (2, 256)
        key = jax.random.key(seed)
        ks = jax.random.split(key, 8)
        s = lambda fan_in: 1.0 / np.sqrt(fan_in)
        return {'x': jax.random.normal(ks[0], (B, T, D_MODEL), jnp.float32), 'wq': jax.random.normal(ks[1], (D_MODEL, N_HEADS * HEAD_DIM), jnp.float32) * s(D_MODEL), 'wk_down': jax.random.normal(ks[2], (D_MODEL, N_KV * D_LAT), jnp.float32) * s(D_MODEL), 'wv_down': jax.random.normal(ks[3], (D_MODEL, N_KV * D_LAT), jnp.float32) * s(D_MODEL), 'wk_up': jax.random.normal(ks[4], (D_LAT, HEAD_DIM), jnp.float32) * s(D_LAT), 'wv_up': jax.random.normal(ks[5], (D_LAT, HEAD_DIM), jnp.float32) * s(D_LAT), 'wo': jax.random.normal(ks[6], (N_HEADS * HEAD_DIM, D_MODEL), jnp.float32) * s(N_HEADS * HEAD_DIM)}
    _L0_attn_in = _L0_attn_setup()

    def _L0_ffn_setup():
        import jax, jax.numpy as jnp
        import numpy as np
        HIDDEN = 128
        N_EXPERTS = 32
        MOE_I = 64
        N_GROUP = 4
        TOPK_GROUP = 2
        TOP_K = 6
        N_LOCAL_GROUPS = 16
        ANCHOR_I = 32
        SHARED_I = 64
        ROUTED_SCALE = 0.2
        ANCHOR_ALPHA = 0.1
        BATCH, SEQ = (1, 128)

        def _moe_forward(hidden_states, gate_weight, gate_bias, w_gate, w_up, w_down, shared_w_gate, shared_w_up, shared_w_down, anchor_w_gate, anchor_w_up, anchor_w_down):
            B, S, H = hidden_states.shape
            x = hidden_states.reshape(-1, H)
            T = x.shape[0]
            E = gate_weight.shape[0]
            L = anchor_w_gate.shape[0]
            logits = x @ gate_weight.T
            scores = jax.nn.sigmoid(logits)
            sc = scores + gate_bias
            grp = sc.reshape(T, N_GROUP, E // N_GROUP)
            group_scores = jax.lax.top_k(grp, 2)[0].sum(-1)
            _, gidx = jax.lax.top_k(group_scores, TOPK_GROUP)
            gmask = jax.nn.one_hot(gidx, N_GROUP, dtype=sc.dtype).sum(1)
            emask = jnp.repeat(gmask, E // N_GROUP, axis=1)
            masked = jnp.where(emask > 0, sc, -jnp.inf)
            _, topidx = jax.lax.top_k(masked, TOP_K)
            tw = jnp.take_along_axis(scores, topidx, axis=-1)
            tw = tw / (tw.sum(-1, keepdims=True) + 1e-20) * ROUTED_SCALE
            g = jnp.einsum('th,ehi->tei', x, w_gate)
            u = jnp.einsum('th,ehi->tei', x, w_up)
            eo = jnp.einsum('tei,eih->teh', jax.nn.silu(g) * u, w_down)
            cw = (jax.nn.one_hot(topidx, E, dtype=x.dtype) * tw[..., None]).sum(1)
            routed = jnp.einsum('te,teh->th', cw, eo)
            shared = jax.nn.silu(x @ shared_w_gate) * (x @ shared_w_up) @ shared_w_down
            lg = topidx[:, 0] // (E // L)
            ag = jnp.einsum('th,lhi->tli', x, anchor_w_gate)
            au = jnp.einsum('th,lhi->tli', x, anchor_w_up)
            ao = jnp.einsum('tli,lih->tlh', jax.nn.silu(ag) * au, anchor_w_down)
            acw = jax.nn.one_hot(lg, L, dtype=x.dtype)
            anchor = jnp.einsum('tl,tlh->th', acw, ao)
            out = routed + shared + ANCHOR_ALPHA * anchor
            return out.reshape(B, S, H)
        key = jax.random.key(seed)
        ks = jax.random.split(key, 13)
        s = 0.02
        return {'hidden_states': jax.random.normal(ks[0], (BATCH, SEQ, HIDDEN), jnp.float32), 'gate_weight': s * jax.random.normal(ks[1], (N_EXPERTS, HIDDEN), jnp.float32), 'gate_bias': s * jax.random.normal(ks[2], (N_EXPERTS,), jnp.float32), 'w_gate': s * jax.random.normal(ks[3], (N_EXPERTS, HIDDEN, MOE_I), jnp.float32), 'w_up': s * jax.random.normal(ks[4], (N_EXPERTS, HIDDEN, MOE_I), jnp.float32), 'w_down': s * jax.random.normal(ks[5], (N_EXPERTS, MOE_I, HIDDEN), jnp.float32), 'shared_w_gate': s * jax.random.normal(ks[6], (HIDDEN, SHARED_I), jnp.float32), 'shared_w_up': s * jax.random.normal(ks[7], (HIDDEN, SHARED_I), jnp.float32), 'shared_w_down': s * jax.random.normal(ks[8], (SHARED_I, HIDDEN), jnp.float32), 'anchor_w_gate': s * jax.random.normal(ks[9], (N_LOCAL_GROUPS, HIDDEN, ANCHOR_I), jnp.float32), 'anchor_w_up': s * jax.random.normal(ks[10], (N_LOCAL_GROUPS, HIDDEN, ANCHOR_I), jnp.float32), 'anchor_w_down': s * jax.random.normal(ks[11], (N_LOCAL_GROUPS, ANCHOR_I, HIDDEN), jnp.float32)}
    _L0_ffn_in = _L0_ffn_setup()
    _d = {'L0_attn_x': _L0_attn_in['x'], 'L0_attn_wq': _L0_attn_in['wq'], 'L0_attn_wk_down': _L0_attn_in['wk_down'], 'L0_attn_wv_down': _L0_attn_in['wv_down'], 'L0_attn_wk_up': _L0_attn_in['wk_up'], 'L0_attn_wv_up': _L0_attn_in['wv_up'], 'L0_attn_wo': _L0_attn_in['wo'], 'L0_ffn_gate_weight': _L0_ffn_in['gate_weight'], 'L0_ffn_gate_bias': _L0_ffn_in['gate_bias'], 'L0_ffn_w_gate': _L0_ffn_in['w_gate'], 'L0_ffn_w_up': _L0_ffn_in['w_up'], 'L0_ffn_w_down': _L0_ffn_in['w_down'], 'L0_ffn_shared_w_gate': _L0_ffn_in['shared_w_gate'], 'L0_ffn_shared_w_up': _L0_ffn_in['shared_w_up'], 'L0_ffn_shared_w_down': _L0_ffn_in['shared_w_down'], 'L0_ffn_anchor_w_gate': _L0_ffn_in['anchor_w_gate'], 'L0_ffn_anchor_w_up': _L0_ffn_in['anchor_w_up'], 'L0_ffn_anchor_w_down': _L0_ffn_in['anchor_w_down']}
    _x0 = _d['L0_attn_x']
    _d['L0_attn_x'] = jax.random.normal(jax.random.fold_in(jax.random.key(seed), 1), (2, 1024, 128), dtype=_x0.dtype)
    del _x0
    return _d

def reference(L0_attn_x, L0_attn_wq, L0_attn_wk_down, L0_attn_wv_down, L0_attn_wk_up, L0_attn_wv_up, L0_attn_wo, L0_ffn_gate_weight, L0_ffn_gate_bias, L0_ffn_w_gate, L0_ffn_w_up, L0_ffn_w_down, L0_ffn_shared_w_gate, L0_ffn_shared_w_up, L0_ffn_shared_w_down, L0_ffn_anchor_w_gate, L0_ffn_anchor_w_up, L0_ffn_anchor_w_down):

    def _L0_attn_ref(x, wq, wk_down, wv_down, wk_up, wv_up, wo):
        import jax, jax.numpy as jnp
        import numpy as np
        D_MODEL, N_HEADS, N_KV, HEAD_DIM, D_LAT = (128, 8, 2, 128, 32)
        N_REP = N_HEADS // N_KV
        B, T = (2, 256)
        Bq, Tq, _ = x.shape
        scale = HEAD_DIM ** (-0.5)
        q = (x @ wq).reshape(Bq, Tq, N_KV, N_REP, HEAD_DIM)
        k_lat = (x @ wk_down).reshape(Bq, Tq, N_KV, D_LAT)
        v_lat = (x @ wv_down).reshape(Bq, Tq, N_KV, D_LAT)
        k = jnp.einsum('bkhl,ld->bkhd', k_lat, wk_up)
        v = jnp.einsum('bkhl,ld->bkhd', v_lat, wv_up)
        scores = jnp.einsum('bqhrd,bkhd->bhrqk', q, k) * scale
        causal = jnp.tril(jnp.ones((Tq, Tq), dtype=bool))
        scores = jnp.where(causal, scores, jnp.finfo(scores.dtype).min)
        probs = jax.nn.softmax(scores, axis=-1)
        y = jnp.einsum('bhrqk,bkhd->bqhrd', probs, v)
        y = y.reshape(Bq, Tq, N_HEADS * HEAD_DIM)
        return y @ wo

    def _L0_ffn_ref(hidden_states, gate_weight, gate_bias, w_gate, w_up, w_down, shared_w_gate, shared_w_up, shared_w_down, anchor_w_gate, anchor_w_up, anchor_w_down):
        import jax, jax.numpy as jnp
        import numpy as np
        HIDDEN = 128
        N_EXPERTS = 32
        MOE_I = 64
        N_GROUP = 4
        TOPK_GROUP = 2
        TOP_K = 6
        N_LOCAL_GROUPS = 16
        ANCHOR_I = 32
        SHARED_I = 64
        ROUTED_SCALE = 0.2
        ANCHOR_ALPHA = 0.1
        BATCH, SEQ = (1, 128)

        def _moe_forward(hidden_states, gate_weight, gate_bias, w_gate, w_up, w_down, shared_w_gate, shared_w_up, shared_w_down, anchor_w_gate, anchor_w_up, anchor_w_down):
            B, S, H = hidden_states.shape
            x = hidden_states.reshape(-1, H)
            T = x.shape[0]
            E = gate_weight.shape[0]
            L = anchor_w_gate.shape[0]
            logits = x @ gate_weight.T
            scores = jax.nn.sigmoid(logits)
            sc = scores + gate_bias
            grp = sc.reshape(T, N_GROUP, E // N_GROUP)
            group_scores = jax.lax.top_k(grp, 2)[0].sum(-1)
            _, gidx = jax.lax.top_k(group_scores, TOPK_GROUP)
            gmask = jax.nn.one_hot(gidx, N_GROUP, dtype=sc.dtype).sum(1)
            emask = jnp.repeat(gmask, E // N_GROUP, axis=1)
            masked = jnp.where(emask > 0, sc, -jnp.inf)
            _, topidx = jax.lax.top_k(masked, TOP_K)
            tw = jnp.take_along_axis(scores, topidx, axis=-1)
            tw = tw / (tw.sum(-1, keepdims=True) + 1e-20) * ROUTED_SCALE
            g = jnp.einsum('th,ehi->tei', x, w_gate)
            u = jnp.einsum('th,ehi->tei', x, w_up)
            eo = jnp.einsum('tei,eih->teh', jax.nn.silu(g) * u, w_down)
            cw = (jax.nn.one_hot(topidx, E, dtype=x.dtype) * tw[..., None]).sum(1)
            routed = jnp.einsum('te,teh->th', cw, eo)
            shared = jax.nn.silu(x @ shared_w_gate) * (x @ shared_w_up) @ shared_w_down
            lg = topidx[:, 0] // (E // L)
            ag = jnp.einsum('th,lhi->tli', x, anchor_w_gate)
            au = jnp.einsum('th,lhi->tli', x, anchor_w_up)
            ao = jnp.einsum('tli,lih->tlh', jax.nn.silu(ag) * au, anchor_w_down)
            acw = jax.nn.one_hot(lg, L, dtype=x.dtype)
            anchor = jnp.einsum('tl,tlh->th', acw, ao)
            out = routed + shared + ANCHOR_ALPHA * anchor
            return out.reshape(B, S, H)
        return _moe_forward(hidden_states, gate_weight, gate_bias, w_gate, w_up, w_down, shared_w_gate, shared_w_up, shared_w_down, anchor_w_gate, anchor_w_up, anchor_w_down)
    x = L0_attn_x
    x = x + _layernorm(_L0_attn_ref(_layernorm(x, axis=-1), L0_attn_wq, L0_attn_wk_down, L0_attn_wv_down, L0_attn_wk_up, L0_attn_wv_up, L0_attn_wo), axis=-1)
    x = x + _layernorm(_L0_ffn_ref(_layernorm(x, axis=-1), L0_ffn_gate_weight, L0_ffn_gate_bias, L0_ffn_w_gate, L0_ffn_w_up, L0_ffn_w_down, L0_ffn_shared_w_gate, L0_ffn_shared_w_up, L0_ffn_shared_w_down, L0_ffn_anchor_w_gate, L0_ffn_anchor_w_up, L0_ffn_anchor_w_down), axis=-1)
    return x

_drawn_inputs = setup_inputs


def setup_inputs(seed=0):
    import zlib

    import numpy as np

    out = dict(_drawn_inputs(seed))
    spreads = {}
    factors = {}
    for name, (base, spread) in spreads.items():
        noise = np.random.default_rng([zlib.crc32(name.encode()), seed]).standard_normal(out[name].shape)
        drawn = base * np.exp(spread * noise) if base else spread * noise
        out[name] = jnp.asarray(drawn.astype(out[name].dtype))
    for name, factor in factors.items():
        out[name] = (out[name] * factor).astype(out[name].dtype)
    return out
```

```python
from contextlib import ExitStack

import concourse.bass as bass
from concourse import mybir

ACT = mybir.ActivationFunctionType
ALU = mybir.AluOpType
AX = mybir.AxisListType
F32 = mybir.dt.float32
F32R = mybir.dt.float32r
BF16 = mybir.dt.bfloat16
U32 = mybir.dt.uint32

P = 128
B, T, D = 2, 1024, 128
HEADS, GROUPS, HD, LAT = 8, 2, 128, 32
REP = HEADS // GROUPS
CH = 512
TPC = CH // P
CPB = T // CH
NCH = B * CPB
NT = B * T // P
SCALE = HD ** -0.5
EPS = 1e-5
QROWS = 3 * LAT
KROWS = QROWS + 3
MASK = -1e30

E, EI = 32, 64
L, LI = 16, 32
SI = 64
EG, ETOP, GTOP = 4, 6, 2
EPG = E // EG
ET, LT = E * EI // P, L * LI // P
MT = ET + LT + 1
WROWS = 3 * E + L
ROUTED_SCALE, ANCHOR_ALPHA = 0.2, 0.1
BIG = 3.0e38
SENTINEL = 3.2e38

BLOCKS = [(b, c, g) for b in range(B) for c in range(CPB) for g in range(GROUPS)]
NB = len(BLOCKS)
SLOTS = 3
QRING = 3


def make_timeline():
    line = []
    slots = 0
    waiting = []

    def flush(every=False):
        while waiting and (every or waiting[0][0] <= slots):
            line.append(waiting.pop(0)[1])

    def slot(ev):
        nonlocal slots
        line.append(ev)
        slots += 1
        if ev[0] == "p2" and ev[3] == 1:
            waiting.append((slots + 2, ("pv", ev[1], ev[2])))
        flush()

    def p1(n):
        return [("p1", n, i, j) for i in range(TPC) for j in range(REP)]

    def p2(n):
        return [("p2", n, kt, p) for kt in range(TPC * (BLOCKS[n][1] + 1)) for p in range(2)]

    line += [("xn", 0), ("setup",), ("xT", 0), ("xn", 1), ("kproj", 0), ("proj", 0), ("vproj", 0), ("proj", 1)]
    for ev in p1(0):
        slot(ev)
    line += [("split", 0), ("rs", 0)]
    line += [("xT", 1), ("shift", 0), ("rb", 0), ("kproj", 1), ("vproj", 1)]
    wsplit = [("wsplit", a, t) for a in range(2) for t in range(0, MT, 3)]
    post = []
    for n in range(NB):
        a, b = p2(n), p1(n + 1) if n + 1 < NB else []
        extra = [("proj", n + 2)] if n + 2 < NB else []
        if n < 2:
            extra += [("xn", n + 2), ("xT", n + 2), ("kproj", n + 2), ("vproj", n + 2)]
        extra += post
        if n >= 2:
            extra += [wsplit.pop(0) for _ in range(min(2, len(wsplit)))]
        post = []
        tail = 4 if len(a) == 8 else 6
        lead = len(a) - tail
        total = len(a) + len(b)
        done_b = 0
        seen = 0
        shifted = not b
        for x, ev in enumerate(a):
            want = len(b) if x >= lead else -(-len(b) * (x + 1) // lead)
            while done_b < want:
                slot(b[done_b])
                done_b += 1
                seen += 1
                if extra and seen % 2 == 0:
                    line.append(extra.pop(0))
            slot(ev)
            seen += 1
            if extra and seen % 2 == 0:
                line.append(extra.pop(0))
            if not shifted and done_b == len(b):
                line.append(("split", n + 1))
                shifted = True
                shift_at = seen + 1
            if b and shifted and seen == shift_at:
                line += [("shift", n + 1), ("rs", n + 1)]
            if b and shifted and seen == shift_at + 2:
                line.append(("rb", n + 1))
        line += extra
        flush(True)
        line.append(("yl", n))
        if BLOCKS[n][2] == GROUPS - 1:
            m = n // GROUPS
            post = [("post_out", m), ("post_T", m), ("post_logits", m), ("route", m), ("post_cwT", m)]
    line += wsplit
    between = {2: post[0], 6: post[1], 9: post[2], 12: post[3], 16: post[4]}
    for m in range(NCH):
        for t in range(MT + 1):
            if t < MT:
                line.append(("gu", m, t))
            if t >= 1:
                line.append(("down", m, t - 1))
            if m == 0 and t in between:
                line.append(between[t])
            if m >= 1 and t == 3:
                line.append(("fin_T", m - 1))
        line.append(("fin_copy", m))
    line.append(("fin_T", NCH - 1))
    return line


TIMELINE = make_timeline()
SLOT = {ev: u for u, ev in enumerate(e for e in TIMELINE if e[0] in ("p1", "p2"))}
MISC_KINDS = ("xT", "kproj", "vproj", "proj", "shift", "rb", "post_out", "post_T", "post_logits", "post_cwT", "fin_T")
MISC = {ev: k for k, ev in enumerate(e for e in TIMELINE if e[0] in MISC_KINDS)}
P1 = {ev: k for k, ev in enumerate(e for e in TIMELINE if e[0] == "p1")}
KT = {ev: k for k, ev in enumerate(e for e in TIMELINE if e[0] == "pv")}
LN_KINDS = ("xn", "post_out", "post_T", "fin_T")
LN = {ev: k for k, ev in enumerate(e for e in TIMELINE if e[0] in ("xn", "post_out", "ln2", "fin_T"))}


WSPLITS = range(0, MT, 3)


def block_kts(n):
    return TPC * (BLOCKS[n][1] + 1)


def build(nc, x, wq, wk_down, wv_down, wk_up, wv_up, wo, gate_weight, gate_bias, w_gate, w_up, w_down,
          shared_w_gate, shared_w_up, shared_w_down, anchor_w_gate, anchor_w_up, anchor_w_down, out):
    with ExitStack() as ctx:
        def sb(name, shape, dt=F32):
            return ctx.enter_context(nc.sbuf_tensor(name, shape, dt))

        def sem(name):
            return ctx.enter_context(nc.semaphore(name))

        x_sb = sb("x_sb", [P, NT, D])
        xT_hi = sb("xT_hi", [P, NT * P], F32R)
        xT_lo = sb("xT_lo", [P, NT * P], F32R)
        kst = sb("kst", [P, GROUPS, B * T], F32R)
        qst = sb("qst", [P, QRING, REP, CH], F32R)
        v_sb = sb("v_sb", [P, NT, GROUPS * LAT])
        q_hi = sb("q_hi", [P, 2, CH], F32R)
        q_lo = sb("q_lo", [P, 2, CH], F32R)
        k_hi = sb("k_hi", [GROUPS * LAT, 2, CH], F32R)
        k_lo = sb("k_lo", [GROUPS * LAT, 2, CH], F32R)
        probs = sb("probs", [P, 2, REP, CH])
        ylat = sb("ylat", [P, GROUPS, CH])
        raw = sb("raw", [P, 3 * HEADS * HD])
        w_hi = sb("w_hi", [P, 2, MT, P], F32R)
        w_lo = sb("w_lo", [P, 2, MT, P], F32R)
        wd = sb("wd", [P, MT, D])
        wkv = sb("wkv", [P, P])
        wkv_hi = sb("wkv_hi", [P, P], F32R)
        wkv_lo = sb("wkv_lo", [P, P], F32R)
        small = sb("small", [E, 3, P])
        smallT = sb("smallT", [P, 3 * E])
        a_s = sb("a_s", [P, HEADS * LAT])
        a_hi = sb("a_hi", [P, HEADS * LAT], F32R)
        a_lo = sb("a_lo", [P, HEADS * LAT], F32R)
        m_sb = sb("m_sb", [P, GROUPS, D])
        gwT_hi = sb("gwT_hi", [P, E], F32R)
        gwT_lo = sb("gwT_lo", [P, E], F32R)
        bias = sb("bias", [P, E])
        ident = sb("ident", [P, P])
        ident_bf = sb("ident_bf", [P, P], BF16)
        mask1 = sb("mask1", [P, P], BF16)
        mask2 = sb("mask2", [P, P], BF16)
        sel = sb("sel", [WROWS, MT - 1, P], BF16)
        anchor_lo = sb("anchor_lo", [P, L])
        lower = sb("lower", [P, EG, EG])
        half = sb("half", [P, 1])
        nmax = sb("nmax", [P, 2, TPC, REP])
        sums = sb("sums", [P, 2, TPC, REP])
        rsum = sb("rsum", [P, TPC, REP])
        rsum_w = sb("rsum_w", [P, TPC, REP, LAT])
        nm_rest = sb("nm_rest", [P, 2, TPC, REP])
        nm3 = sb("nm3", [P, TPC, 3, REP], BF16)
        shift_rows = sb("shift_rows", [3 * REP, 2, CH], F32R)
        rb = sb("rb", [P, 2, CH])
        stats = sb("stats", [P, TPC, 6])
        mv = sb("mv", [P, TPC, 2])
        var_eps = sb("var_eps", [P, TPC])
        rstd = sb("rstd", [P, TPC])
        normed = sb("normed", [P, TPC, D])
        enx = sb("enx", [P, TPC, E])
        score = sb("score", [P, TPC, E])
        biased = sb("biased", [P, TPC, E])
        top_g = sb("top_g", [P, TPC, EG, 8])
        gscore = sb("gscore", [P, TPC, EG])
        above = sb("above", [P, TPC, EG, EG])
        ties = sb("ties", [P, TPC, EG, EG])
        rank = sb("rank", [P, TPC, EG])
        gtake = sb("gtake", [P, TPC, EG])
        gout = sb("gout", [P, TPC, EG])
        cand = sb("cand", [P, TPC, E + 2])
        cand_rep = sb("cand_rep", [P, TPC, E + 2])
        top8 = sb("top8", [P, TPC, 8])
        top_at = sb("top_at", [P, TPC, 8], U32)
        best = sb("best", [P, TPC])
        wsum = sb("wsum", [P, TPC])
        cw = sb("cw", [P, 2, TPC, E])
        dist = sb("dist", [P, 2, TPC, L])
        weights = sb("weights", [P, TPC, WROWS], BF16)
        cwT = sb("cwT", [WROWS, NCH, CH], BF16)
        moe = probs[:].rearrange("p a j n -> p (a j) n")
        oT = moe[:, 6, :]
        y_out = ylat[:].rearrange("p r (t d) -> p r t d", d=D)

        wq_sb = raw[:, 0:HEADS * HD]
        wo_sb = raw[:, HEADS * HD:2 * HEADS * HD].rearrange("p (h d) -> p h d", d=D)
        wqT = raw[:, 2 * HEADS * HD:3 * HEADS * HD].rearrange("p (h d) -> p h d", d=D)
        w_raw = raw[:, 0:MT * P].rearrange("p (t c) -> p t c", c=P)

        ps = ctx.enter_context(nc.psum_tensor("ps", [P, 6, CH], F32))
        acc = ctx.enter_context(nc.psum_tensor("acc", [P, CH], F32))
        misc = ctx.enter_context(nc.psum_tensor("misc", [P, CH], F32))
        misc_bf = misc[:].bitcast(BF16)

        def slot(u):
            return ps[:, 2 * (u % SLOTS):2 * (u % SLOTS) + 2, :]

        x_in = [sem(f"x_in{c}") for c in range(NCH)]
        attn_w_in = sem("attn_w_in")
        bias_in = sem("bias_in")
        gu_w_in = sem("gu_w_in")
        down_w_in = sem("down_w_in")
        consts = sem("consts")
        var_ready = sem("var_ready")
        rstd_ready = sem("rstd_ready")
        xn_ready = sem("xn_ready")
        wT_full = sem("wT_full")
        wqT_ready = sem("wqT_ready")
        small_ready = sem("small_ready")
        am_full = sem("am_full")
        setup_done = sem("setup_done")
        misc_full = sem("misc_full")
        misc_free = sem("misc_free")
        hi_ready = sem("hi_ready")
        lo_ready = sem("lo_ready")
        k_in = [sem(f"k_in{c}") for c in range(NCH)]
        q_in = [sem(f"q_in{r}") for r in range(QRING)]
        shift_in = [sem(f"shift_in{r}") for r in range(QRING)]
        slot_full = sem("slot_full")
        slot_free = sem("slot_free")
        nmax_ready = sem("nmax_ready")
        nm3_ready = sem("nm3_ready")
        rsum_ready = sem("rsum_ready")
        shift_ready = sem("shift_ready")
        pv_done = sem("pv_done")
        ylat_ready = sem("ylat_ready")
        logits_read = sem("logits_read")
        weights_ready = sem("weights_ready")
        cwT_ready = sem("cwT_ready")
        split_done = sem("split_done")
        anchors_scaled = sem("anchors_scaled")
        gu_full = sem("gu_full")
        silu_ready = sem("silu_ready")
        h_ready = sem("h_ready")
        down_done = sem("down_done")
        oT_ready = sem("oT_ready")
        y_ready = sem("y_ready")
        y_stored = [sem(f"y_stored{r}") for r in range(2)]
        vec_link = sem("vec_link")
        pool_link = sem("pool_link")

        HILO = {ev: k for k, ev in enumerate(e for e in TIMELINE if e[0] in ("xT", "kproj", "proj", "post_T"))}
        XN = {ev: k for k, ev in enumerate(e for e in TIMELINE if e[0] in ("xn", "post_T"))}

        def ln_events():
            for ev in TIMELINE:
                if ev[0] in ("xn", "fin_T"):
                    yield ev
                if ev[0] == "post_out":
                    yield ev
                    yield ("ln2", ev[1])
        LNK = {ev: k for k, ev in enumerate(ln_events())}
        CHAINS = [ev for ev in TIMELINE if ev[0] in ("p1", "p2")]

        x_rows = x.rearrange("b t d -> (b t) d").rearrange("(n p) d -> p n d", p=P)
        out_rows = out.rearrange("b t d -> (b t) d").rearrange("(n p) d -> p n d", p=P)

        block = ctx.enter_context(nc.Block())

        @block.sync
        def _(sp):
            def load_inner(experts, anchors, shared):
                sp.dma_start(w_raw[:, 0:ET, :].rearrange("p t (e i) -> p (t e) i", i=EI), experts.rearrange("e d i -> d e i")).then_inc(gu_w_in, 16)
                sp.dma_start(w_raw[:, ET:ET + LT, :].rearrange("p t (e i) -> p (t e) i", i=LI), anchors.rearrange("e d i -> d e i")).then_inc(gu_w_in, 16)
                for r in range(2):
                    sp.dma_start(w_raw[:, MT - 1, SI * r:SI * r + SI], shared).then_inc(gu_w_in, 16)

            for c in range(NCH):
                if c == 1:
                    sp.dma_start(small[:, 0, :], wk_up).then_inc(attn_w_in, 16)
                    sp.dma_start(small[:, 1, :], wv_up).then_inc(attn_w_in, 16)
                    sp.dma_start(small[:, 2, :], gate_weight).then_inc(attn_w_in, 16)
                    sp.dma_start(wq_sb, wq).then_inc(attn_w_in, 16)
                    sp.dma_start(wo_sb, wo.rearrange("(h p) d -> p h d", p=P)).then_inc(attn_w_in, 16)
                    sp.dma_start(wkv[:, 0:GROUPS * LAT], wk_down).then_inc(attn_w_in, 16)
                    sp.dma_start(wkv[:, GROUPS * LAT:], wv_down).then_inc(attn_w_in, 16)
                sp.dma_start(x_sb[:, TPC * c:TPC * c + TPC, :], x_rows[:, TPC * c:TPC * c + TPC, :]).then_inc(x_in[c], 16)
            sp.dma_start(bias[:], gate_bias.partition_broadcast(P)).then_inc(bias_in, 16)
            sp.dma_start(wd[:, 0:ET, :], w_down.rearrange("e i d -> (e i) d").rearrange("(t p) d -> p t d", p=P)).then_inc(down_w_in, 16)
            sp.dma_start(wd[:, ET:ET + LT, :], anchor_w_down.rearrange("e i d -> (e i) d").rearrange("(t p) d -> p t d", p=P)).then_inc(down_w_in, 16)
            sp.dma_start(wd[0:SI, MT - 1, :], shared_w_down).then_inc(down_w_in, 16)
            for ev in TIMELINE:
                kind = ev[0]
                if kind == "setup":
                    sp.wait_ge(setup_done, 1)
                    load_inner(w_gate, anchor_w_gate, shared_w_gate)
                elif kind == "wsplit" and ev[1:] == (0, WSPLITS[-1]):
                    sp.wait_ge(split_done, len(WSPLITS))
                    load_inner(w_up, anchor_w_up, shared_w_up)
                elif kind == "kproj":
                    c = ev[1]
                    sp.wait_ge(lo_ready, HILO[ev] + 1)
                    for g in range(GROUPS):
                        rows = slice(LAT * g, LAT * g + LAT)
                        for r, part in enumerate((k_hi, k_lo, k_hi)):
                            sp.dma_start(kst[LAT * r:LAT * r + LAT, g, CH * c:CH * c + CH].bitcast(F32), part[rows, c % 2, :].bitcast(F32)).then_inc(k_in[c], 16)
                elif kind == "proj":
                    n = ev[1]
                    sp.wait_ge(lo_ready, HILO[ev] + 1)
                    if n >= QRING:
                        last = n - QRING
                        sp.wait_ge(slot_full, SLOT["p2", last, block_kts(last) - 1, 1] + 1)
                    for r, part in enumerate((q_hi, q_hi, q_lo)):
                        for j in range(REP):
                            sp.dma_start(qst[LAT * r:LAT * r + LAT, n % QRING, j, :].bitcast(F32), part[LAT * j:LAT * j + LAT, n % 2, :].bitcast(F32)).then_inc(q_in[n % QRING], 16)
                elif kind == "shift":
                    n = ev[1]
                    sp.wait_ge(shift_ready, n + 1)
                    for r in range(3):
                        sp.dma_start(qst[QROWS + r:QROWS + r + 1, n % QRING, :, :].bitcast(F32), shift_rows[REP * r:REP * r + REP, n % 2, :].bitcast(F32)).then_inc(shift_in[n % QRING], 16)
                elif kind == "fin_T":
                    m = ev[1]
                    sp.wait_ge(y_ready, m + 1)
                    sp.dma_start(out_rows[:, TPC * m:TPC * m + TPC, :], y_out[:, m % 2]).then_inc(y_stored[m % 2], 16)
            for r in range(2):
                sp.wait_ge(y_stored[r], 16 * (NCH // 2))

        @block.gpsimd
        def _(pool):
            links = [0]

            def link(ins):
                links[0] += 1
                ins.then_inc(pool_link, 1)
                pool.wait_ge(pool_link, links[0])

            link(nc.gpsimd.memset(ident[:], 0.0))
            nc.gpsimd.affine_select(out=ident[:], in_=ident[:], compare_op=ALU.not_equal, fill=1.0, base=0,
                                    pattern=[[-1, P]], channel_multiplier=1).then_inc(consts, 1)
            nc.gpsimd.memset(half[:], -0.5).then_inc(consts, 1)

            def rstd_of(ev):
                pool.wait_ge(var_ready, LNK[ev] + 1)
                link(nc.gpsimd.tensor_scalar(var_eps[:], mv[:, :, 1], EPS, None, ALU.add))
                nc.gpsimd.tensor_tensor(rstd[:], var_eps[:], half[:].to_broadcast([P, TPC]), ALU.pow).then_inc(rstd_ready, 1)

            pool.wait_ge(consts, 2)
            rstd_of(("xn", 0))
            link(nc.gpsimd.memset(ident_bf[:], 0.0))
            nc.gpsimd.affine_select(out=ident_bf[:], in_=ident_bf[:], compare_op=ALU.not_equal, fill=1.0, base=0,
                                    pattern=[[-1, P]], channel_multiplier=1).then_inc(consts, 1)
            link(nc.gpsimd.memset(mask1[:], 0.0))
            nc.gpsimd.affine_select(out=mask1[:], in_=mask1[:], compare_op=ALU.is_ge, fill=MASK, base=0,
                                    pattern=[[-1, P]], channel_multiplier=1).then_inc(consts, 1)
            link(nc.gpsimd.memset(mask2[:], 0.0))
            nc.gpsimd.affine_select(out=mask2[:], in_=mask2[:], compare_op=ALU.is_ge, fill=MASK, base=0,
                                    pattern=[[1, P]], channel_multiplier=-1).then_inc(consts, 1)
            pool.wait_ge(consts, 5)
            nc.gpsimd.memset(kst[QROWS:KROWS, :, :].bitcast(F32), 1.0).then_inc(consts, 1)
            pool.wait_ge(consts, 6)
            rstd_of(("xn", 1))
            link(nc.gpsimd.memset(sel[:], 0.0))
            for part in range(3):
                v = sel[:, 0:ET, :].rearrange("p t (e i) -> p t e i", e=2)
                link(nc.gpsimd.affine_select(out=v, in_=v, compare_op=ALU.not_equal, fill=1.0, base=-E * part,
                                             pattern=[[-2, ET], [-1, 2], [0, EI]], channel_multiplier=1))
            v = sel[:, ET:ET + LT, :].rearrange("p t (e i) -> p t e i", e=P // LI)
            nc.gpsimd.affine_select(out=v, in_=v, compare_op=ALU.not_equal, fill=1.0, base=-3 * E,
                                    pattern=[[-(P // LI), LT], [-1, P // LI], [0, LI]], channel_multiplier=1).then_inc(consts, 1)
            nc.gpsimd.iota(anchor_lo[:], pattern=[[E // L, L]], base=0, channel_multiplier=0,
                           allow_small_or_imprecise_dtypes=True).then_inc(consts, 1)
            link(nc.gpsimd.memset(lower[:], 0.0))
            nc.gpsimd.affine_select(out=lower[:], in_=lower[:], compare_op=ALU.is_ge, fill=1.0, base=0,
                                    pattern=[[-1, EG], [1, EG]], channel_multiplier=0).then_inc(consts, 1)
            nc.gpsimd.memset(cand[:, :, E:E + 2], SENTINEL).then_inc(consts, 1)
            pool.wait_ge(down_w_in, 48)
            nc.gpsimd.tensor_scalar(wd[:, ET:ET + LT, :], wd[:, ET:ET + LT, :], ANCHOR_ALPHA, None, ALU.mult).then_inc(anchors_scaled, 1)
            for ev in ln_events():
                if ev not in (("xn", 0), ("xn", 1)):
                    rstd_of(ev)
        CONSTS = 10

        @block.scalar
        def _(act):
            def evacuate_hi(ev, dst, src):
                act.wait_ge(misc_full, MISC[ev] + 1)
                nc.scalar.activation(dst, src, ACT.Copy).then_inc(hi_ready, 1)

            for ev in TIMELINE:
                kind = ev[0]
                if kind == "setup":
                    act.wait_ge(wT_full, 1)
                    nc.scalar.activation(wqT, ps[:, 0:2, :].rearrange("p a (h d) -> p (a h) d", d=D), ACT.Copy).then_inc(wqT_ready, 1)
                elif kind in ("xT", "post_T"):
                    c = ev[1]
                    evacuate_hi(ev, xT_hi[:, CH * c:CH * c + CH], misc[:])
                elif kind == "kproj":
                    c = ev[1]
                    if c >= 2:
                        act.wait_ge(k_in[c - 2], 16 * 3 * GROUPS)
                    evacuate_hi(ev, k_hi[:, c % 2, :], misc[0:GROUPS * LAT, :])
                elif kind == "proj":
                    n = ev[1]
                    if n >= 2:
                        act.wait_ge(q_in[(n - 2) % QRING], 16 * 3 * REP * ((n - 2) // QRING + 1))
                    evacuate_hi(ev, q_hi[:, n % 2, :], misc[:])
                elif kind == "p1":
                    _, n, i, j = ev
                    u = SLOT[ev]
                    keys = CH * BLOCKS[n][1] + P * (i + 1)
                    s = slot(u).rearrange("p a n -> p (a n)")[:, 0:keys]
                    act.wait_ge(nmax_ready, P1[ev] + 1)
                    nc.scalar.activation(s, s, ACT.Exp, bias=nmax[:, n % 2, i, j:j + 1],
                                         accum_out=sums[:, n % 2, i, j:j + 1]).then_inc(slot_free, 1)
                elif kind == "p2":
                    _, n, kt, p = ev
                    u = SLOT[ev]
                    off = P * max(0, kt - TPC * BLOCKS[n][1])
                    k = KT["pv", n, kt]
                    act.wait_ge(slot_full, u + 1)
                    if k >= 2:
                        act.wait_ge(pv_done, k - 1)
                    nc.scalar.activation(probs[:, k % 2, 2 * p:2 * p + 2, off:CH], slot(u)[:, :, 0:CH - off], ACT.Exp).then_inc(slot_free, 1)
                elif kind == "post_logits":
                    act.wait_ge(misc_full, MISC[ev] + 1)
                    nc.scalar.activation(enx[:].rearrange("p t e -> p (t e)"), misc[:, 0:TPC * E], ACT.Exp, scale=-1.0).then_inc(logits_read, 1)
                elif kind == "gu":
                    _, m, t = ev
                    k = MT * m + t
                    rows = SI if t == MT - 1 else P
                    act.wait_ge(gu_full, k + 1)
                    if k == 0:
                        act.wait_ge(pv_done, len(KT))
                    nc.scalar.activation(moe[0:rows, k % 2, :], ps[0:rows, 3 * (k % 2), :], ACT.Silu).then_inc(silu_ready, 1)
                elif kind == "fin_copy":
                    m = ev[1]
                    act.wait_ge(down_done, MT * (m + 1))
                    if m >= 1:
                        act.wait_ge(misc_full, MISC["fin_T", m - 1] + 1)
                    nc.scalar.activation(oT, acc[:], ACT.Copy).then_inc(oT_ready, 1)

        @block.vector
        def _(dve):
            links = [0]

            def link(ins):
                links[0] += 1
                ins.then_inc(vec_link, 1)
                dve.wait_ge(vec_link, links[0])

            def moments(ev, src):
                for t in range(TPC):
                    last = nc.vector.bn_stats(stats[:, t, :], src[:, t, :])
                link(last)
                for t in range(TPC):
                    last = nc.vector.bn_aggr(mv[:, t, :], stats[:, t, :])
                last.then_inc(var_ready, 1)
                dve.wait_ge(rstd_ready, LNK[ev] + 1)

            def normalise(dst, src):
                for t in range(TPC):
                    last = nc.vector.tensor_scalar(dst[:, t, :], src[:, t, :], mv[:, t, 0:1], rstd[:, t:t + 1],
                                                   ALU.subtract, ALU.mult)
                return last

            def evacuate_lo(ev, dst, src, hi):
                dve.wait_ge(misc_full, MISC[ev] + 1)
                dve.wait_ge(hi_ready, HILO[ev] + 1)
                nc.vector.tensor_tensor(dst, src, hi.bitcast(F32), ALU.subtract).then_inc(lo_ready, 1)

            def halves(dst_hi, dst_lo, src):
                link(nc.vector.tensor_copy(dst_hi, src))
                return nc.vector.tensor_tensor(dst_lo, src, dst_hi.bitcast(F32), ALU.subtract)

            for ev in TIMELINE:
                kind = ev[0]
                if kind == "xn":
                    c = ev[1]
                    rows = x_sb[:, TPC * c:TPC * c + TPC, :]
                    dve.wait_ge(x_in[c], 16)
                    moments(ev, rows)
                    if c >= 1:
                        dve.wait_ge(misc_full, MISC["xT", c - 1] + 1)
                    normalise(normed, rows).then_inc(xn_ready, 1)
                elif kind == "setup":
                    dve.wait_ge(wT_full, 2)
                    nc.vector.tensor_copy(smallT[:], misc[:, 0:3 * E]).then_inc(small_ready, 1)
                    dve.wait_ge(attn_w_in, 16 * 7)
                    link(halves(wkv_hi[:], wkv_lo[:], wkv[:]))
                    dve.wait_ge(small_ready, 1)
                    link(halves(gwT_hi[:], gwT_lo[:], smallT[:, 2 * E:3 * E]))
                    dve.wait_ge(am_full, 1)
                    link(nc.vector.tensor_scalar(a_s[:], ps[:, 2, 0:HEADS * LAT], SCALE, None, ALU.mult))
                    link(nc.vector.tensor_copy(m_sb[:].rearrange("p g d -> p (g d)"), ps[:, 3, 0:GROUPS * D]))
                    halves(a_hi[:], a_lo[:], a_s[:]).then_inc(setup_done, 1)
                elif kind == "xT":
                    c = ev[1]
                    evacuate_lo(ev, xT_lo[:, CH * c:CH * c + CH], misc[:], xT_hi[:, CH * c:CH * c + CH])
                elif kind == "kproj":
                    c = ev[1]
                    evacuate_lo(ev, k_lo[:, c % 2, :], misc[0:GROUPS * LAT, :], k_hi[:, c % 2, :])
                elif kind == "proj":
                    n = ev[1]
                    evacuate_lo(ev, q_lo[:, n % 2, :], misc[:], q_hi[:, n % 2, :])
                elif kind == "vproj":
                    c = ev[1]
                    dve.wait_ge(misc_full, MISC[ev] + 1)
                    nc.vector.tensor_copy(v_sb[:, TPC * c:TPC * c + TPC, :].rearrange("p t l -> p (t l)"),
                                          misc[:, 0:TPC * GROUPS * LAT]).then_inc(misc_free, 1)
                elif kind == "p1":
                    _, n, i, j = ev
                    u = SLOT[ev]
                    keys = CH * BLOCKS[n][1] + P * (i + 1)
                    dve.wait_ge(slot_full, u + 1)
                    nc.vector.tensor_reduce(nmax[:, n % 2, i, j:j + 1], slot(u).rearrange("p a n -> p (a n)")[:, 0:keys],
                                            AX.X, ALU.max, negate=True).then_inc(nmax_ready, 1)
                elif kind == "split":
                    n = ev[1]
                    dve.wait_ge(nmax_ready, P1["p1", n, TPC - 1, REP - 1] + 1)
                    if n >= 1:
                        dve.wait_ge(misc_full, MISC["shift", n - 1] + 1)
                    left = nmax[:, n % 2]
                    for part in range(3):
                        ins = nc.vector.tensor_copy(nm3[:, :, part, :], left)
                        if part == 2:
                            ins.then_inc(nm3_ready, 1)
                            break
                        link(ins)
                        link(nc.vector.tensor_tensor(nm_rest[:, part], left, nm3[:, :, part, :], ALU.subtract))
                        left = nm_rest[:, part]
                elif kind == "shift":
                    n = ev[1]
                    dve.wait_ge(misc_full, MISC[ev] + 1)
                    if n >= 2:
                        dve.wait_ge(shift_in[(n - 2) % QRING], 48 * ((n - 2) // QRING + 1))
                    nc.vector.tensor_copy(shift_rows[:, n % 2, :], misc[0:3 * REP, :]).then_inc(shift_ready, 1)
                elif kind == "rs":
                    n = ev[1]
                    dve.wait_ge(slot_free, SLOT["p1", n, TPC - 1, REP - 1] + 1)
                    link(nc.vector.reciprocal(rsum[:], sums[:, n % 2]))
                    if n >= 1:
                        dve.wait_ge(misc_full, MISC["rb", n - 1] + 1)
                    nc.vector.tensor_copy(rsum_w[:], rsum[:].unsqueeze(3).to_broadcast([P, TPC, REP, LAT])).then_inc(rsum_ready, 1)
                elif kind == "rb":
                    n = ev[1]
                    dve.wait_ge(misc_full, MISC[ev] + 1)
                    if n >= 2:
                        dve.wait_ge(ylat_ready, n - 1)
                    nc.vector.tensor_copy(rb[:, n % 2, :], misc[:]).then_inc(misc_free, 1)
                elif kind == "yl":
                    n = ev[1]
                    b, c, g = BLOCKS[n]
                    dve.wait_ge(pv_done, KT["pv", n, block_kts(n) - 1] + 1)
                    dve.wait_ge(misc_free, FREED["rb", n] + 1)
                    if n >= GROUPS:
                        dve.wait_ge(misc_full, MISC["post_out", n // GROUPS - 1] + 1)
                    nc.vector.tensor_tensor(ylat[:, g, :], acc[:], rb[:, n % 2, :], ALU.mult).then_inc(ylat_ready, 1)
                elif kind == "post_out":
                    m = ev[1]
                    rows = x_sb[:, TPC * m:TPC * m + TPC, :]
                    o = misc[:].rearrange("p (t d) -> p t d", d=D)
                    dve.wait_ge(misc_full, MISC[ev] + 1)
                    moments(ev, o)
                    if m >= 1:
                        dve.wait_ge(misc_full, MISC["post_T", m - 1] + 1)
                    normalise(normed, o).then_inc(misc_free, 1)
                    dve.wait_ge(misc_free, FREED[ev] + 1)
                    link(nc.vector.tensor_tensor(rows, rows, normed[:], ALU.add))
                    moments(("ln2", m), rows)
                    normalise(normed, rows).then_inc(xn_ready, 1)
                elif kind == "post_T":
                    m = ev[1]
                    evacuate_lo(ev, xT_lo[:, CH * m:CH * m + CH], misc[:], xT_hi[:, CH * m:CH * m + CH])
                elif kind == "route":
                    m = ev[1]
                    dve.wait_ge(logits_read, m + 1)
                    dve.wait_ge(consts, CONSTS)
                    dve.wait_ge(bias_in, 16)
                    link(nc.vector.tensor_scalar(score[:], enx[:], 1.0, None, ALU.add))
                    link(nc.vector.reciprocal(score[:], score[:]))
                    link(nc.vector.tensor_tensor(biased[:], score[:], bias[:].unsqueeze(1).to_broadcast([P, TPC, E]), ALU.add))
                    for t in range(TPC):
                        for g in range(EG):
                            last = nc.vector.max(top_g[:, t, g, :], biased[:, t, EPG * g:EPG * g + EPG])
                    link(last)
                    link(nc.vector.tensor_tensor(gscore[:], top_g[:, :, :, 0], top_g[:, :, :, 1], ALU.add))
                    other = gscore[:].unsqueeze(2).to_broadcast([P, TPC, EG, EG])
                    own = gscore[:].unsqueeze(3).to_broadcast([P, TPC, EG, EG])
                    nc.vector.tensor_tensor(above[:], other, own, ALU.is_gt)
                    link(nc.vector.tensor_tensor(ties[:], other, own, ALU.is_equal))
                    link(nc.vector.tensor_tensor(ties[:], ties[:], lower[:].unsqueeze(1).to_broadcast([P, TPC, EG, EG]), ALU.mult))
                    link(nc.vector.tensor_tensor(above[:], above[:], ties[:], ALU.add))
                    link(nc.vector.tensor_reduce(rank[:], above[:], AX.X, ALU.add))
                    link(nc.vector.tensor_scalar(gtake[:], rank[:], float(GTOP), None, ALU.is_lt))
                    nc.vector.tensor_scalar(gout[:], gtake[:], 1.0, BIG, ALU.subtract, ALU.mult)
                    link(nc.vector.tensor_tensor(biased[:].rearrange("p t (g e) -> p t g e", e=EPG),
                                                 biased[:].rearrange("p t (g e) -> p t g e", e=EPG),
                                                 gtake[:].unsqueeze(3).to_broadcast([P, TPC, EG, EPG]), ALU.mult))
                    link(nc.vector.tensor_tensor(cand[:, :, 0:E].rearrange("p t (g e) -> p t g e", e=EPG),
                                                 biased[:].rearrange("p t (g e) -> p t g e", e=EPG),
                                                 gout[:].unsqueeze(3).to_broadcast([P, TPC, EG, EPG]), ALU.add))
                    for t in range(TPC):
                        last = nc.vector.max(top8[:, t, :], cand[:, t, :])
                    link(last)
                    for t in range(TPC):
                        nc.vector.max_index(top_at[:, t, :], top8[:, t, :], cand[:, t, :])
                        last = nc.vector.match_replace(cand_rep[:, t, :], top8[:, t, :], cand[:, t, :], -SENTINEL)
                    link(last)
                    link(nc.vector.tensor_tensor(cw[:, 0], cand_rep[:, :, 0:E], cand[:, :, 0:E], ALU.not_equal))
                    link(nc.vector.tensor_tensor(score[:], score[:], cw[:, 0], ALU.mult))
                    link(nc.vector.tensor_reduce(wsum[:], score[:], AX.X, ALU.add))
                    link(nc.vector.tensor_scalar(wsum[:], wsum[:], 1e-20, None, ALU.add))
                    link(nc.vector.reciprocal(wsum[:], wsum[:]))
                    link(nc.vector.scalar_tensor_tensor(cw[:, 0], score[:], ROUTED_SCALE, wsum[:].unsqueeze(2).to_broadcast([P, TPC, E]),
                                                        ALU.mult, ALU.mult))
                    if m >= 1:
                        dve.wait_ge(misc_full, MISC["post_cwT", m - 1] + 1)
                    for part in range(3):
                        link(nc.vector.tensor_copy(weights[:, :, E * part:E * part + E], cw[:, part % 2]))
                        if part < 2:
                            link(nc.vector.tensor_tensor(cw[:, (part + 1) % 2], cw[:, part % 2],
                                                         weights[:, :, E * part:E * part + E], ALU.subtract))
                    link(nc.vector.tensor_copy(best[:], top_at[:, :, 2]))
                    link(nc.vector.tensor_tensor(dist[:, 0], best[:].unsqueeze(2).to_broadcast([P, TPC, L]),
                                                 anchor_lo[:].unsqueeze(1).to_broadcast([P, TPC, L]), ALU.subtract))
                    link(nc.vector.tensor_scalar(dist[:, 1], dist[:, 0], 0.0, None, ALU.is_ge))
                    nc.vector.scalar_tensor_tensor(weights[:, :, 3 * E:WROWS], dist[:, 0], float(E // L), dist[:, 1],
                                                   ALU.is_lt, ALU.mult).then_inc(weights_ready, 1)
                elif kind == "post_cwT":
                    m = ev[1]
                    dve.wait_ge(misc_full, MISC[ev] + 1)
                    nc.vector.tensor_copy(cwT[:, m, :], misc_bf[0:WROWS, 0:CH]).then_inc(cwT_ready, 1)
                elif kind == "wsplit":
                    _, a, t = ev
                    if t == 0:
                        dve.wait_ge(gu_w_in, 16 * 4 * (a + 1))
                    ts = slice(t, min(MT, t + 3))
                    halves(w_hi[:, a, ts, :], w_lo[:, a, ts, :], w_raw[:, ts, :]).then_inc(split_done, 1)
                elif kind == "gu":
                    _, m, t = ev
                    k = MT * m + t
                    rows = SI if t == MT - 1 else P
                    bank = 3 * (k % 2)
                    dve.wait_ge(silu_ready, k + 1)
                    if k >= 2:
                        dve.wait_ge(down_done, k - 1)
                    if t == MT - 1:
                        nc.vector.tensor_tensor(moe[0:rows, 4 + k % 2, :], moe[0:rows, k % 2, :], ps[0:rows, bank + 1, :], ALU.mult).then_inc(h_ready, 1)
                    else:
                        link(nc.vector.tensor_tensor(moe[:, 2 + k % 2, :], moe[:, k % 2, :], ps[:, bank + 1, :], ALU.mult))
                        nc.vector.tensor_tensor(moe[:, 4 + k % 2, :], moe[:, 2 + k % 2, :], ps[:, bank + 2, :], ALU.mult).then_inc(h_ready, 1)
                elif kind == "fin_T":
                    m = ev[1]
                    o = misc[:].rearrange("p (t d) -> p t d", d=D)
                    dve.wait_ge(misc_full, MISC[ev] + 1)
                    moments(ev, o)
                    normalise(normed, o).then_inc(misc_free, 1)
                    dve.wait_ge(misc_free, FREED[ev] + 1)
                    if m >= 2:
                        dve.wait_ge(y_stored[m % 2], 16 * (m // 2))
                    nc.vector.tensor_tensor(y_out[:, m % 2], x_sb[:, TPC * m:TPC * m + TPC, :], normed[:], ALU.add).then_inc(y_ready, 1)

        @block.tensor
        def _(pe):
            def misc_turn(ev):
                k = MISC[ev]
                if k == 0:
                    pe.wait_ge(small_ready, 1)
                    return
                before = MISC_ORDER[k - 1]
                if before[0] in ("xT", "kproj", "proj", "post_T"):
                    pe.wait_ge(lo_ready, HILO[before] + 1)
                elif before[0] == "shift":
                    pe.wait_ge(shift_ready, before[1] + 1)
                elif before[0] == "post_logits":
                    pe.wait_ge(logits_read, before[1] + 1)
                elif before[0] == "post_cwT":
                    pe.wait_ge(cwT_ready, before[1] + 1)
                else:
                    pe.wait_ge(misc_free, FREED[before] + 1)

            def three(dst, lhs, rhs):
                nc.tensor.matmul(dst, lhs[0], rhs[0], start=True, stop=False)
                nc.tensor.matmul(dst, lhs[0], rhs[1], start=False, stop=False)
                return nc.tensor.matmul(dst, lhs[1], rhs[0], start=False, stop=True)

            started = [False]
            for ev in TIMELINE:
                kind = ev[0]
                if kind == "setup":
                    pe.wait_ge(consts, 1)
                    pe.wait_ge(attn_w_in, 16 * 7)
                    for h in range(HEADS):
                        last = nc.tensor.transpose(ps[:, h // 4, D * (h % 4):D * (h % 4) + D], wq_sb[:, HD * h:HD * h + HD], ident[:])
                    last.then_inc(wT_full, 1)
                    for r in range(3):
                        last = nc.tensor.transpose(misc[:, E * r:E * r + E], small[:, r, :], ident[0:E, 0:E])
                    last.then_inc(wT_full, 1)
                    pe.wait_ge(wqT_ready, 1)
                    pe.wait_ge(small_ready, 1)
                    for h in range(HEADS):
                        nc.tensor.matmul(ps[:, 2, LAT * h:LAT * h + LAT], wqT[:, h, :], smallT[:, 0:LAT], start=True, stop=True)
                    for h in range(HEADS):
                        g, j = h // REP, h % REP
                        last = nc.tensor.matmul(ps[LAT * j:LAT * j + LAT, 3, D * g:D * g + D], smallT[:, E:E + LAT], wo_sb[:, h, :], start=True, stop=True)
                    last.then_inc(am_full, 1)
                elif kind in ("xT", "post_T"):
                    pe.wait_ge(xn_ready, XN_OF[ev] + 1)
                    misc_turn(ev)
                    for t in range(TPC):
                        last = nc.tensor.transpose(misc[:, P * t:P * t + P], normed[:, t, :], ident[:])
                    last.then_inc(misc_full, 1)
                elif kind == "kproj":
                    c = ev[1]
                    cols = slice(CH * c, CH * c + CH)
                    misc_turn(ev)
                    if c == 0:
                        pe.wait_ge(setup_done, 1)
                    pe.wait_ge(lo_ready, HILO["xT", c] + 1)
                    three(misc[:], (wkv_hi[:], wkv_lo[:]), (xT_hi[:, cols], xT_lo[:, cols])).then_inc(misc_full, 1)
                elif kind == "vproj":
                    c = ev[1]
                    misc_turn(ev)
                    wv = slice(GROUPS * LAT, 2 * GROUPS * LAT)
                    for t in range(TPC):
                        cols = slice(CH * c + P * t, CH * c + P * t + P)
                        last = three(misc[:, GROUPS * LAT * t:GROUPS * LAT * (t + 1)], (xT_hi[:, cols], xT_lo[:, cols]), (wkv_hi[:, wv], wkv_lo[:, wv]))
                    last.then_inc(misc_full, 1)
                elif kind == "proj":
                    n = ev[1]
                    b, c, g = BLOCKS[n]
                    m = CPB * b + c
                    cols = slice(CH * m, CH * m + CH)
                    heads = slice(REP * LAT * g, REP * LAT * (g + 1))
                    misc_turn(ev)
                    pe.wait_ge(lo_ready, HILO["xT", m] + 1)
                    three(misc[:], (a_hi[:, heads], a_lo[:, heads]), (xT_hi[:, cols], xT_lo[:, cols])).then_inc(misc_full, 1)
                elif kind == "p1":
                    _, n, i, j = ev
                    b, c, g = BLOCKS[n]
                    u = SLOT[ev]
                    keys = CH * c + P * (i + 1)
                    if (i, j) == (0, 0):
                        pe.wait_ge(q_in[n % QRING], 16 * 3 * REP * (n // QRING + 1))
                        for cc in range(c + 1):
                            pe.wait_ge(k_in[CPB * b + cc], 16 * 3 * GROUPS)
                        pe.wait_ge(consts, 6)
                    if u >= SLOTS:
                        pe.wait_ge(slot_free, u - SLOTS + 1)
                    lhs = qst[0:QROWS, n % QRING, j, P * i:P * i + P]
                    for h in range(c + 1):
                        width = min(CH, keys - CH * h)
                        at = T * b + CH * h
                        nc.tensor.matmul(slot(u)[:, h, 0:width], lhs, kst[0:QROWS, g, at:at + width], start=True, stop=(h < c))
                    nc.tensor.matmul(slot(u)[:, c, P * i:P * i + P], ident_bf[:], mask1[:], start=False, stop=True).then_inc(slot_full, 1)
                elif kind == "shift":
                    n = ev[1]
                    misc_turn(ev)
                    pe.wait_ge(nm3_ready, n + 1)
                    for i in range(TPC):
                        last = nc.tensor.matmul(misc[0:3 * REP, P * i:P * i + P], nm3[:, i].rearrange("p a j -> p (a j)"), ident_bf[:], start=True, stop=True)
                    last.then_inc(misc_full, 1)
                elif kind == "rb":
                    n = ev[1]
                    misc_turn(ev)
                    pe.wait_ge(rsum_ready, n + 1)
                    for i in range(TPC):
                        last = nc.tensor.transpose(misc[:, P * i:P * i + P], rsum_w[:, i].rearrange("p j l -> p (j l)"), ident[:])
                    last.then_inc(misc_full, 1)
                elif kind == "p2":
                    _, n, kt, p = ev
                    b, c, g = BLOCKS[n]
                    u = SLOT[ev]
                    diag = kt >= TPC * c
                    off = P * max(0, kt - TPC * c)
                    if (kt, p) == (0, 0):
                        pe.wait_ge(shift_in[n % QRING], 48 * (n // QRING + 1))
                    pe.wait_ge(slot_free, u - SLOTS + 1)
                    at = T * b + P * kt
                    for r in range(2):
                        j = 2 * p + r
                        last = nc.tensor.matmul(slot(u)[:, r, 0:CH - off], kst[0:KROWS, g, at:at + P], qst[0:KROWS, n % QRING, j, off:CH], start=True, stop=not diag)
                        if diag:
                            last = nc.tensor.matmul(slot(u)[:, r, 0:P], ident_bf[:], mask2[:], start=False, stop=True)
                    last.then_inc(slot_full, 1)
                elif kind == "pv":
                    _, n, kt = ev
                    b, c, g = BLOCKS[n]
                    k = KT[ev]
                    off = P * max(0, kt - TPC * c)
                    pe.wait_ge(slot_free, SLOT["p2", n, kt, 1] + 1)
                    if kt == 0 and n >= 1:
                        pe.wait_ge(ylat_ready, n)
                    if kt == 0:
                        for cc in range(c + 1):
                            pe.wait_ge(misc_free, FREED["vproj", CPB * b + cc] + 1)
                    for j in range(REP):
                        last = nc.tensor.matmul(acc[LAT * j:LAT * j + LAT, off:CH], v_sb[:, (T // P) * b + kt, LAT * g:LAT * g + LAT], probs[:, k % 2, j, off:CH],
                                                start=(kt == 0), stop=(kt == block_kts(n) - 1))
                    last.then_inc(pv_done, 1)
                elif kind == "post_out":
                    m = ev[1]
                    misc_turn(ev)
                    pe.wait_ge(ylat_ready, GROUPS * (m + 1))
                    for t in range(TPC):
                        for g in range(GROUPS):
                            last = nc.tensor.matmul(misc[:, D * t:D * t + D], ylat[:, g, P * t:P * t + P], m_sb[:, g, :], start=(g == 0), stop=(g == GROUPS - 1))
                    last.then_inc(misc_full, 1)
                elif kind == "post_logits":
                    m = ev[1]
                    misc_turn(ev)
                    pe.wait_ge(lo_ready, HILO["post_T", m] + 1)
                    for t in range(TPC):
                        cols = slice(CH * m + P * t, CH * m + P * t + P)
                        last = three(misc[:, E * t:E * t + E], (xT_hi[:, cols], xT_lo[:, cols]), (gwT_hi[:], gwT_lo[:]))
                    last.then_inc(misc_full, 1)
                elif kind == "post_cwT":
                    m = ev[1]
                    misc_turn(ev)
                    pe.wait_ge(weights_ready, m + 1)
                    for t in range(TPC):
                        last = nc.tensor.transpose(misc_bf[0:WROWS, P * t:P * t + P], weights[:, t, :], ident_bf[:])
                    last.then_inc(misc_full, 1)
                elif kind == "gu":
                    _, m, t = ev
                    k = MT * m + t
                    bank = 3 * (k % 2)
                    cols = slice(CH * m, CH * m + CH)
                    if k == 0:
                        pe.wait_ge(split_done, 2 * len(WSPLITS))
                        pe.wait_ge(slot_free, len(SLOT))
                    if t == 0:
                        pe.wait_ge(cwT_ready, m + 1)
                        pe.wait_ge(consts, CONSTS)
                    if k >= 2:
                        pe.wait_ge(h_ready, k - 1)
                    for a in range(2):
                        last = three(ps[:, bank + a, :], (w_hi[:, a, t, :], w_lo[:, a, t, :]), (xT_hi[:, cols], xT_lo[:, cols]))
                    if t < MT - 1:
                        last = nc.tensor.matmul(ps[:, bank + 2, :], sel[:, t, :], cwT[:, m, :], start=True, stop=True)
                    last.then_inc(gu_full, 1)
                elif kind == "down":
                    _, m, t = ev
                    k = MT * m + t
                    rows = SI if t == MT - 1 else P
                    pe.wait_ge(h_ready, k + 1)
                    if k == 0:
                        pe.wait_ge(anchors_scaled, 1)
                        pe.wait_ge(ylat_ready, NB)
                    if t == 0 and m >= 1:
                        pe.wait_ge(oT_ready, m)
                    nc.tensor.matmul(acc[:], wd[0:rows, t, :], moe[0:rows, 4 + k % 2, :], start=(t == 0), stop=(t == MT - 1)).then_inc(down_done, 1)
                elif kind == "fin_T":
                    m = ev[1]
                    misc_turn(ev)
                    pe.wait_ge(oT_ready, m + 1)
                    for t in range(TPC):
                        last = nc.tensor.transpose(misc[:, P * t:P * t + P], oT[:, P * t:P * t + P], ident[:])
                    last.then_inc(misc_full, 1)


MISC_ORDER = sorted(MISC, key=MISC.get)
FREED = {ev: k for k, ev in enumerate(e for e in MISC_ORDER if e[0] in ("vproj", "rb", "post_out", "fin_T"))}
XN_OF = {}
for _ev in TIMELINE:
    if _ev[0] == "xn":
        XN_OF["xT", _ev[1]] = len(XN_OF)
    if _ev[0] == "post_out":
        XN_OF["post_T", _ev[1]] = len(XN_OF)

_NAMES = ["attn_x", "attn_wq", "attn_wk_down", "attn_wv_down", "attn_wk_up", "attn_wv_up", "attn_wo", "ffn_gate_weight", "ffn_gate_bias",
          "ffn_w_gate", "ffn_w_up", "ffn_w_down", "ffn_shared_w_gate", "ffn_shared_w_up", "ffn_shared_w_down", "ffn_anchor_w_gate",
          "ffn_anchor_w_up", "ffn_anchor_w_down"]


def kernel(**inputs):
    import numpy as np
    import concourse.bacc as bacc
    from concourse.bass_utils import run_bass_kernel_spmd

    nc = bacc.Bacc("TRN2", target_bir_lowering=False, num_devices=1)
    arrays, args = {}, []
    for name in _NAMES:
        a = np.ascontiguousarray(inputs[f"L0_{name}"])
        arrays[f"in_{name}"] = a
        args.append(nc.dram_tensor(f"in_{name}", a.shape, mybir.dt.from_np(a.dtype), kind="ExternalInput").ap())
    args.append(nc.dram_tensor("result", (B, T, D), F32, kind="ExternalOutput").ap())
    build(nc, *args)
    r = run_bass_kernel_spmd(nc, [arrays], core_ids=[0])
    return r.results[0]["result"]
```

```python
from contextlib import ExitStack

import concourse.bass as bass
from concourse import mybir

ACT = mybir.ActivationFunctionType
ALU = mybir.AluOpType
AX = mybir.AxisListType
F32 = mybir.dt.float32
F32R = mybir.dt.float32r
BF16 = mybir.dt.bfloat16
U32 = mybir.dt.uint32

P = 128
B, T, D = 2, 1024, 128
HEADS, GROUPS, HD, LAT = 8, 2, 128, 32
REP = HEADS // GROUPS
CH = 512
TPC = CH // P
CPB = T // CH
NCH = B * CPB
NT = B * T // P
SCALE = HD ** -0.5
EPS = 1e-5
QROWS = 3 * LAT
KROWS = QROWS + 3
MASK = -1e30

E, EI = 32, 64
L, LI = 16, 32
SI = 64
EG, ETOP, GTOP = 4, 6, 2
EPG = E // EG
ET, LT = E * EI // P, L * LI // P
MT = ET + LT + 1
WROWS = 3 * E + L
ROUTED_SCALE, ANCHOR_ALPHA = 0.2, 0.1
BIG = 3.0e38
SENTINEL = 3.2e38

CHUNKS = [(b, c if b == 0 else CPB - 1 - c) for b in range(B) for c in range(CPB)]
CHUNK = [CPB * b + c for b, c in CHUNKS]
BLOCKS = [(b, c, g) for b, c in CHUNKS for g in range(GROUPS)]
NB = len(BLOCKS)
SBANKS = 6
KTBUF = 3
EXP_LAG = 0
TAIL = 4
PV_LAG = 3
PV_STEP = 2
YL_LAG = 1
QRING = 3


MISC_KINDS = ("xT", "kproj", "vproj", "proj", "shift", "rb", "post_out", "post_T", "post_logits", "post_cwT", "fin_T")
ROUTE_STEPS = 9
PACE = 3
QUIET = ("load", "scale", "wsplit", "post_add", "fin_add")
TAKES = {"xn_mom": {"ln"}, "post_out": {"ln", "misc", "post"}, "fin_T": {"ln", "misc"}}
GIVES = {"xT": {"ln"}, "post_nrm": {"misc"}, "post_T": {"ln"}, "post_cwT": {"post"}, "fin_nrm": {"misc"}, "fin_add": {"ln"}}


def make_timeline():
    line = []
    slots = 0
    held = set()
    agenda = []

    def put(ev):
        line.append(ev)
        held.update(TAKES.get(ev[0], ()))
        held.difference_update(GIVES.get(ev[0], ()))

    def chain(*steps):
        agenda.append([slots + steps[0][0], list(steps)])

    def may(ev):
        needs = set(TAKES.get(ev[0], ()))
        if ev[0] in MISC_KINDS:
            needs.add("misc")
        return not needs & held

    def tick(limit=1, tensor=True):
        for c in list(agenda):
            while c[1] and c[0] <= slots and may(c[1][0][1]):
                ev = c[1][0][1]
                loud = ev[0] not in QUIET
                if loud and (limit == 0 or (ev[0] in MISC_KINDS and not tensor)):
                    break
                limit -= loud
                put(ev)
                c[1].pop(0)
                if c[1]:
                    c[0] = slots + c[1][0][0]
            if not c[1]:
                agenda.remove(c)

    def until(ev):
        nonlocal slots
        while ev not in line:
            slots += 1
            tick(2)

    def product():
        ev = pvs.pop(0)[1]
        n, kt, h = ev[1:]
        if n >= 1 and (kt, h) == (0, 0):
            until(("yl", n - 1))
        put(ev)
        if (kt, h) == (block_kts(n) - 1, 1):
            until(("rb", n))
            if n >= GROUPS:
                until(("post_out", n // GROUPS - 1))
            steps = [(YL_LAG, ("yl", n))]
            if BLOCKS[n][2] == GROUPS - 1:
                steps += post(n // GROUPS)
            agenda.insert(0, [slots + steps[0][0], steps])

    def slot(ev):
        nonlocal slots
        pair = ev if ev[0] == "pair" else None
        if pair:
            n = pair[1][1]
            until(("proj", n))
            for c in range(BLOCKS[n][1] + 1):
                until(("kproj", BLOCKS[n][0] * CPB + c))
            for step in pair[1:]:
                put(step)
        else:
            until(("shift", ev[1]))
            put(ev)
        slots += 1
        if pair:
            exps.append([slots + EXP_LAG, pair])
            if pair == p1(n)[-1]:
                scale = [(1, ("scale", n))] if BLOCKS[n][1] else []
                agenda.insert(0, [slots + EXP_LAG, [(0, ("split", n)), (1, ("shift", n)), *scale, (1, ("rs", n)), (2, ("rb", n))]])
        while exps and exps[0][0] <= slots:
            for step in exps.pop(0)[1][1:]:
                put(("exp", *step[1:]))
        if ev[0] == "p2" and ev[3] == 1:
            pvs.extend([slots + PV_LAG + PV_STEP * h, ("pv", ev[1], ev[2], h)] for h in range(2))
        due = bool(pvs) and pvs[0][0] <= slots
        if due:
            product()
        tick(1, not due)

    def post(m):
        return ([(1, ("post_out", m)), (2, ("post_mom", m)), (2, ("post_nrm", m)), (0, ("post_add", m)), (PACE, ("post_mom2", m)),
                 (PACE, ("post_nrm2", m)), (PACE, ("post_T", m)), (PACE, ("post_logits", m))]
                + [(PACE, ("route", m, r)) for r in range(ROUTE_STEPS)] + [(PACE, ("post_cwT", m))])

    def tokens(c):
        return [(1, ("xn_mom", c)), (2, ("xn_nrm", c)), (2, ("xT", c)), (2, ("kproj", c)), (2, ("vproj", c))]

    pvs = []
    exps = []

    def p1(n):
        c = BLOCKS[n][1]
        steps = [("p1", n, i, j, h) for i in range(TPC) for j in range(REP) for h in range(c + 1)]
        return [("pair", *steps[k:k + 2]) for k in range(0, len(steps), 2)]

    for ev in [("xn_mom", 0), ("xn_nrm", 0), ("xT", 0), ("setup_T",), ("kproj", 0), ("setup_am",), ("proj", 0), ("vproj", 0), ("load", 0)]:
        put(ev)
    chain((2, ("proj", 1)))
    chain(*tokens(1))
    chain(*tokens(2), *tokens(3))
    p1s = [ev for n in range(NB) for ev in p1(n)]
    p2s = [[("p2", n, kt, p) for kt in range(block_kts(n)) for p in range(2)] for n in range(NB)]
    done = 0

    def lead(upto):
        nonlocal done
        while done < upto:
            slot(p1s[done])
            done += 1

    lead(len(p1(0)))
    at, mark, goal = 0, 0, len(p1(0))
    for n in range(NB):
        if n in (2, 4):
            which = n // 2 - 1
            chain(*[(2, ("wsplit", which, t)) for t in range(0, MT, 3)], *([(0, ("load", 1))] if which == 0 else []))
        for x, ev in enumerate(p2s[n]):
            left = len(p2s[n]) - x
            if x == 0 and n == 0:
                agenda.insert(0, [slots + 3, [(0, ("proj", 2))]])
            if left == TAIL // 2 and n + 3 < NB:
                agenda.insert(0, [slots, [(0, ("proj", n + 3))]])
            if left == TAIL and n >= 0:
                mark, goal = at, goal + (len(p1(n + 1)) if n + 1 < NB else 0)
            slot(ev)
            at += 1
            step = n if left > TAIL else n + 1
            more = len(p1(step + 1)) if step + 1 < NB else 0
            span = len(p2s[0]) - TAIL if step == 0 else len(p2s[min(step, NB - 1)])
            lead(goal + -(-more * (at - mark) // span))
    while pvs:
        slots += 1
        product()
    while any(c[1][0][1][0] == "yl" for c in agenda):
        slots += 1
        tick()
    for k in range(NCH * MT + 2):
        if k < NCH * MT:
            until(("post_cwT", k // MT))
            put(("gu", k // MT, k % MT))
        if k >= 2:
            m, t = divmod(k - 2, MT)
            put(("down", m, t))
            if t == MT - 1:
                put(("fin_copy", m))
                chain((2, ("fin_T", m)), (3, ("fin_mom", m)), (2, ("fin_nrm", m)), (0, ("fin_add", m)))
        slots += 2
        tick()
    while agenda:
        slots += 1
        tick()
    return line


def block_kts(n):
    return TPC * (BLOCKS[n][1] + 1)


TIMELINE = make_timeline()
SLOT = {ev: u for u, ev in enumerate(e for e in TIMELINE if e[0] in ("p1", "p2"))}
EXP = {("p1" if ev[0] == "exp" else "p2", *ev[1:]): k for k, ev in enumerate(e for e in TIMELINE if e[0] in ("exp", "p2"))}
P1_LAST = {ev[1]: ev for ev in SLOT if ev[0] == "p1"}


def place_scores():
    bank, before, users, at = {}, {}, [0] * SBANKS, 0
    for ev in SLOT:
        width = 2 if ev[0] == "p2" else 1
        assert at % width == 0
        bank[ev] = at
        before[ev] = max(users[at:at + width])
        users[at:at + width] = [EXP[ev] + 1] * width
        at = (at + width) % SBANKS
    return bank, before


BANK, EXPS_BEFORE = place_scores()
MISC = {ev: k for k, ev in enumerate(e for e in TIMELINE if e[0] in MISC_KINDS)}
P1 = {ev: k for k, ev in enumerate(e for e in TIMELINE if e[0] == "p1")}
PV = {ev: k for k, ev in enumerate(e for e in TIMELINE if e[0] == "pv")}
LN = {ev: k for k, ev in enumerate(e for e in TIMELINE if e[0] in ("xn_mom", "post_mom", "post_mom2", "fin_mom"))}


WSPLITS = range(0, MT, 3)


def build(nc, x, wq, wk_down, wv_down, wk_up, wv_up, wo, gate_weight, gate_bias, w_gate, w_up, w_down,
          shared_w_gate, shared_w_up, shared_w_down, anchor_w_gate, anchor_w_up, anchor_w_down, out):
    with ExitStack() as ctx:
        def sb(name, shape, dt=F32):
            return ctx.enter_context(nc.sbuf_tensor(name, shape, dt))

        def sem(name):
            return ctx.enter_context(nc.semaphore(name))

        x_sb = sb("x_sb", [P, NT, D])
        xT_hi = sb("xT_hi", [P, NT * P], F32R)
        xT_lo = sb("xT_lo", [P, NT * P], F32R)
        kst = sb("kst", [P, GROUPS, B * T], F32R)
        qst = sb("qst", [P, QRING, REP, CH], F32R)
        v_sb = sb("v_sb", [P, NT, GROUPS * LAT])
        q_hi = sb("q_hi", [P, CH], F32R)
        q_lo = sb("q_lo", [P, CH], F32R)
        k_hi = sb("k_hi", [GROUPS * LAT, CH], F32R)
        k_lo = sb("k_lo", [GROUPS * LAT, CH], F32R)
        probs = sb("probs", [P, KTBUF, REP, CH])
        ylat = sb("ylat", [P, GROUPS, CH])
        raw = sb("raw", [P, 3 * HEADS * HD])
        w_hi = sb("w_hi", [P, 2, MT, P], F32R)
        w_lo = sb("w_lo", [P, 2, MT, P], F32R)
        wd = sb("wd", [P, MT, D])
        wkv = sb("wkv", [P, P])
        wkv_hi = sb("wkv_hi", [P, P], F32R)
        wkv_lo = sb("wkv_lo", [P, P], F32R)
        small = sb("small", [E, 3, P])
        smallT = sb("smallT", [P, 3 * E])
        a_s = sb("a_s", [P, HEADS * LAT])
        a_hi = sb("a_hi", [P, HEADS * LAT], F32R)
        a_lo = sb("a_lo", [P, HEADS * LAT], F32R)
        m_sb = sb("m_sb", [P, GROUPS, D])
        gwT_hi = sb("gwT_hi", [P, E], F32R)
        gwT_lo = sb("gwT_lo", [P, E], F32R)
        bias = sb("bias", [P, E])
        ident = sb("ident", [P, P])
        ident_bf = sb("ident_bf", [P, P], BF16)
        mask1 = sb("mask1", [P, P], BF16)
        mask2 = sb("mask2", [P, P], BF16)
        sel = sb("sel", [WROWS, MT - 1, P], BF16)
        anchor_lo = sb("anchor_lo", [P, L])
        lower = sb("lower", [P, EG, EG])
        half = sb("half", [P, 1])
        nmax_h = sb("nmax_h", [P, 2, TPC, REP, CPB])
        sums_h = sb("sums_h", [P, 2, TPC, REP, CPB])
        nmax = sb("nmax", [P, TPC, REP])
        scales = sb("scales", [P, TPC, REP, CPB])
        scaled = sb("scaled", [P, TPC, REP, CPB])
        sums = sb("sums", [P, TPC, REP])
        rsum = sb("rsum", [P, TPC, REP])
        rsum_w = sb("rsum_w", [P, TPC, REP, LAT])
        nm_rest = sb("nm_rest", [P, 2, TPC, REP])
        nm3 = sb("nm3", [P, TPC, 3, REP], BF16)
        shift_rows = sb("shift_rows", [3 * REP, 2, CH], F32R)
        rb = sb("rb", [P, 2, CH])
        stats = sb("stats", [P, TPC, 6])
        mv = sb("mv", [P, TPC, 2])
        var_eps = sb("var_eps", [P, TPC])
        rstd = sb("rstd", [P, TPC])
        normed = sb("normed", [P, TPC, D])
        enx = sb("enx", [P, TPC, E])
        score = sb("score", [P, TPC, E])
        biased = sb("biased", [P, TPC, E])
        top_g = sb("top_g", [P, TPC, EG, 8])
        gscore = sb("gscore", [P, TPC, EG])
        above = sb("above", [P, TPC, EG, EG])
        ties = sb("ties", [P, TPC, EG, EG])
        rank = sb("rank", [P, TPC, EG])
        gtake = sb("gtake", [P, TPC, EG])
        gout = sb("gout", [P, TPC, EG])
        cand = sb("cand", [P, TPC, E + 2])
        cand_rep = sb("cand_rep", [P, TPC, E + 2])
        top8 = sb("top8", [P, TPC, 8])
        top_at = sb("top_at", [P, TPC, 8], U32)
        best = sb("best", [P, TPC])
        wsum = sb("wsum", [P, TPC])
        cw = sb("cw", [P, 2, TPC, E])
        dist = sb("dist", [P, 2, TPC, L])
        weights = sb("weights", [P, TPC, WROWS], BF16)
        cwT = sb("cwT", [WROWS, NCH, CH], BF16)
        moe = probs[:].rearrange("p a j n -> p (a j) n")
        oT = moe[:, 6, :]
        y_out = moe[:, 8:10, :].rearrange("p r (t d) -> p r t d", d=D)

        wq_sb = raw[:, 0:HEADS * HD]
        wo_sb = raw[:, HEADS * HD:2 * HEADS * HD].rearrange("p (h d) -> p h d", d=D)
        wqT = raw[:, 2 * HEADS * HD:3 * HEADS * HD].rearrange("p (h d) -> p h d", d=D)
        w_raw = raw[:, 0:MT * P].rearrange("p (t c) -> p t c", c=P)

        ps = ctx.enter_context(nc.psum_tensor("ps", [P, 6, CH], F32))
        acc = ctx.enter_context(nc.psum_tensor("acc", [P, CH], F32))
        misc = ctx.enter_context(nc.psum_tensor("misc", [P, CH], F32))
        misc_bf = misc[:].bitcast(BF16)

        def keys_of(ev):
            _, n, i, j, h = ev
            return CH if h < BLOCKS[n][1] else P * (i + 1)

        x_in = [sem(f"x_in{c}") for c in range(NCH)]
        kv_w_in = sem("kv_w_in")
        up_w_in = sem("up_w_in")
        attn_w_in = sem("attn_w_in")
        bias_in = sem("bias_in")
        gu_w_in = sem("gu_w_in")
        down_w_in = sem("down_w_in")
        consts = sem("consts")
        var_ready = sem("var_ready")
        rstd_ready = sem("rstd_ready")
        normed_ready = sem("normed_ready")
        wT_full = sem("wT_full")
        wqT_ready = sem("wqT_ready")
        small_ready = sem("small_ready")
        am_full = sem("am_full")
        setup_done = sem("setup_done")
        wkv_ready = sem("wkv_ready")
        resid_ready = sem("resid_ready")
        misc_full = sem("misc_full")
        misc_free = sem("misc_free")
        hi_ready = sem("hi_ready")
        lo_ready = sem("lo_ready")
        k_in = [sem(f"k_in{c}") for c in range(NCH)]
        q_in = [sem(f"q_in{r}") for r in range(QRING)]
        shift_in = [sem(f"shift_in{r}") for r in range(QRING)]
        slot_full = sem("slot_full")
        slot_free = sem("slot_free")
        nmax_ready = sem("nmax_ready")
        scales_due = sem("scales_due")
        scales_ready = sem("scales_ready")
        nm3_ready = sem("nm3_ready")
        rsum_ready = sem("rsum_ready")
        shift_ready = sem("shift_ready")
        pv_done = sem("pv_done")
        ylat_ready = sem("ylat_ready")
        logits_read = sem("logits_read")
        weights_ready = sem("weights_ready")
        cwT_ready = sem("cwT_ready")
        split_done = sem("split_done")
        anchors_scaled = sem("anchors_scaled")
        gu_full = sem("gu_full")
        silu_ready = sem("silu_ready")
        h_ready = sem("h_ready")
        down_done = sem("down_done")
        oT_ready = sem("oT_ready")
        y_ready = sem("y_ready")
        y_stored = [sem(f"y_stored{r}") for r in range(2)]
        vec_link = sem("vec_link")
        pool_link = sem("pool_link")

        HILO = {ev: k for k, ev in enumerate(e for e in TIMELINE if e[0] in ("xT", "kproj", "proj", "post_T"))}
        x_rows = x.rearrange("b t d -> (b t) d").rearrange("(n p) d -> p n d", p=P)
        out_rows = out.rearrange("b t d -> (b t) d").rearrange("(n p) d -> p n d", p=P)

        block = ctx.enter_context(nc.Block())

        @block.sync
        def _(sp):
            def load_inner(experts, anchors, shared):
                sp.dma_start(w_raw[:, 0:ET, :].rearrange("p t (e i) -> p (t e) i", i=EI), experts.rearrange("e d i -> d e i")).then_inc(gu_w_in, 16)
                sp.dma_start(w_raw[:, ET:ET + LT, :].rearrange("p t (e i) -> p (t e) i", i=LI), anchors.rearrange("e d i -> d e i")).then_inc(gu_w_in, 16)
                for r in range(2):
                    sp.dma_start(w_raw[:, MT - 1, SI * r:SI * r + SI], shared).then_inc(gu_w_in, 16)

            for c in range(NCH):
                if c == 1:
                    sp.dma_start(wkv[:, 0:GROUPS * LAT], wk_down).then_inc(kv_w_in, 16)
                    sp.dma_start(wkv[:, GROUPS * LAT:], wv_down).then_inc(kv_w_in, 16)
                    sp.dma_start(small[:, 0, :], wk_up).then_inc(up_w_in, 16)
                    sp.dma_start(small[:, 1, :], wv_up).then_inc(up_w_in, 16)
                    sp.dma_start(small[:, 2, :], gate_weight).then_inc(up_w_in, 16)
                    sp.dma_start(wq_sb, wq).then_inc(attn_w_in, 16)
                    sp.dma_start(wo_sb, wo.rearrange("(h p) d -> p h d", p=P)).then_inc(attn_w_in, 16)
                sp.dma_start(x_sb[:, TPC * c:TPC * c + TPC, :], x_rows[:, TPC * c:TPC * c + TPC, :]).then_inc(x_in[c], 16)
            sp.dma_start(bias[:], gate_bias.partition_broadcast(P)).then_inc(bias_in, 16)
            sp.dma_start(wd[:, 0:ET, :], w_down.rearrange("e i d -> (e i) d").rearrange("(t p) d -> p t d", p=P)).then_inc(down_w_in, 16)
            sp.dma_start(wd[:, ET:ET + LT, :], anchor_w_down.rearrange("e i d -> (e i) d").rearrange("(t p) d -> p t d", p=P)).then_inc(down_w_in, 16)
            sp.dma_start(wd[0:SI, MT - 1, :], shared_w_down).then_inc(down_w_in, 16)
            for ev in TIMELINE:
                kind = ev[0]
                if ev == ("load", 0):
                    sp.wait_ge(setup_done, 1)
                    load_inner(w_gate, anchor_w_gate, shared_w_gate)
                elif ev == ("load", 1):
                    sp.wait_ge(split_done, len(WSPLITS))
                    load_inner(w_up, anchor_w_up, shared_w_up)
                elif kind == "kproj":
                    c = ev[1]
                    sp.wait_ge(lo_ready, HILO[ev] + 1)
                    for g in range(GROUPS):
                        rows = slice(LAT * g, LAT * g + LAT)
                        for r, part in enumerate((k_hi, k_lo, k_hi)):
                            sp.dma_start(kst[LAT * r:LAT * r + LAT, g, CH * c:CH * c + CH].bitcast(F32), part[rows, :].bitcast(F32)).then_inc(k_in[c], 16)
                elif kind == "proj":
                    n = ev[1]
                    sp.wait_ge(lo_ready, HILO[ev] + 1)
                    if n >= QRING:
                        last = n - QRING
                        sp.wait_ge(slot_full, SLOT["p2", last, block_kts(last) - 1, 1] + 1)
                    for r, part in enumerate((q_hi, q_hi, q_lo)):
                        for j in range(REP):
                            sp.dma_start(qst[LAT * r:LAT * r + LAT, n % QRING, j, :].bitcast(F32), part[LAT * j:LAT * j + LAT, :].bitcast(F32)).then_inc(q_in[n % QRING], 16)
                elif kind == "fin_add":
                    m = ev[1]
                    sp.wait_ge(y_ready, m + 1)
                    sp.dma_start(out_rows[:, TPC * CHUNK[m]:TPC * CHUNK[m] + TPC, :], y_out[:, m % 2]).then_inc(y_stored[m % 2], 16)
            for r in range(2):
                sp.wait_ge(y_stored[r], 16 * (NCH // 2))

        @block.gpsimd
        def _(pool):
            links = [0]

            def link(ins):
                links[0] += 1
                ins.then_inc(pool_link, 1)
                pool.wait_ge(pool_link, links[0])

            link(nc.gpsimd.memset(ident[:], 0.0))
            nc.gpsimd.affine_select(out=ident[:], in_=ident[:], compare_op=ALU.not_equal, fill=1.0, base=0,
                                    pattern=[[-1, P]], channel_multiplier=1).then_inc(consts, 1)
            nc.gpsimd.memset(half[:], -0.5).then_inc(consts, 1)

            def rstd_of(ev):
                pool.wait_ge(var_ready, LN[ev] + 1)
                link(nc.gpsimd.tensor_scalar(var_eps[:], mv[:, :, 1], EPS, None, ALU.add))
                nc.gpsimd.tensor_tensor(rstd[:], var_eps[:], half[:].to_broadcast([P, TPC]), ALU.pow).then_inc(rstd_ready, 1)

            pool.wait_ge(consts, 2)
            rstd_of(("xn_mom", 0))
            link(nc.gpsimd.memset(ident_bf[:], 0.0))
            nc.gpsimd.affine_select(out=ident_bf[:], in_=ident_bf[:], compare_op=ALU.not_equal, fill=1.0, base=0,
                                    pattern=[[-1, P]], channel_multiplier=1).then_inc(consts, 1)
            link(nc.gpsimd.memset(mask1[:], 0.0))
            nc.gpsimd.affine_select(out=mask1[:], in_=mask1[:], compare_op=ALU.is_ge, fill=MASK, base=0,
                                    pattern=[[-1, P]], channel_multiplier=1).then_inc(consts, 1)
            link(nc.gpsimd.memset(mask2[:], 0.0))
            nc.gpsimd.affine_select(out=mask2[:], in_=mask2[:], compare_op=ALU.is_ge, fill=MASK, base=0,
                                    pattern=[[1, P]], channel_multiplier=-1).then_inc(consts, 1)
            pool.wait_ge(consts, 5)
            nc.gpsimd.memset(kst[QROWS:KROWS, :, :].bitcast(F32), 1.0).then_inc(consts, 1)
            pool.wait_ge(consts, 6)
            rstd_of(("xn_mom", 1))
            link(nc.gpsimd.memset(sel[:], 0.0))
            for part in range(3):
                v = sel[:, 0:ET, :].rearrange("p t (e i) -> p t e i", e=2)
                link(nc.gpsimd.affine_select(out=v, in_=v, compare_op=ALU.not_equal, fill=1.0, base=-E * part,
                                             pattern=[[-2, ET], [-1, 2], [0, EI]], channel_multiplier=1))
            v = sel[:, ET:ET + LT, :].rearrange("p t (e i) -> p t e i", e=P // LI)
            nc.gpsimd.affine_select(out=v, in_=v, compare_op=ALU.not_equal, fill=1.0, base=-3 * E,
                                    pattern=[[-(P // LI), LT], [-1, P // LI], [0, LI]], channel_multiplier=1).then_inc(consts, 1)
            nc.gpsimd.iota(anchor_lo[:], pattern=[[E // L, L]], base=0, channel_multiplier=0,
                           allow_small_or_imprecise_dtypes=True).then_inc(consts, 1)
            link(nc.gpsimd.memset(lower[:], 0.0))
            nc.gpsimd.affine_select(out=lower[:], in_=lower[:], compare_op=ALU.is_ge, fill=1.0, base=0,
                                    pattern=[[-1, EG], [1, EG]], channel_multiplier=0).then_inc(consts, 1)
            nc.gpsimd.memset(cand[:, :, E:E + 2], SENTINEL).then_inc(consts, 1)
            pool.wait_ge(down_w_in, 48)
            nc.gpsimd.tensor_scalar(wd[:, ET:ET + LT, :], wd[:, ET:ET + LT, :], ANCHOR_ALPHA, None, ALU.mult).then_inc(anchors_scaled, 1)
            for ev in TIMELINE:
                kind = ev[0]
                if ev in LN and ev not in (("xn_mom", 0), ("xn_mom", 1)):
                    rstd_of(ev)
                elif kind == "shift":
                    n = ev[1]
                    pool.wait_ge(shift_ready, n + 1)
                    for r in range(3):
                        pool.dma_start(qst[QROWS + r:QROWS + r + 1, n % QRING, :, :].bitcast(F32), shift_rows[REP * r:REP * r + REP, n % 2, :].bitcast(F32)).then_inc(shift_in[n % QRING], 16)
                elif kind == "post_add":
                    m = ev[1]
                    rows = x_sb[:, TPC * CHUNK[m]:TPC * CHUNK[m] + TPC, :]
                    pool.wait_ge(normed_ready, NORMED["post_nrm", m] + 1)
                    nc.gpsimd.tensor_tensor(rows, rows, normed[:], ALU.add).then_inc(resid_ready, 1)
                elif kind == "fin_add":
                    m = ev[1]
                    pool.wait_ge(normed_ready, NORMED["fin_nrm", m] + 1)
                    if m >= 2:
                        pool.wait_ge(y_stored[m % 2], 16 * (m // 2))
                    nc.gpsimd.tensor_tensor(y_out[:, m % 2], x_sb[:, TPC * CHUNK[m]:TPC * CHUNK[m] + TPC, :], normed[:], ALU.add).then_inc(y_ready, 1)
                elif kind == "wsplit":
                    _, a, t = ev
                    if t == 0:
                        pool.wait_ge(gu_w_in, 16 * 4 * (a + 1))
                    ts = slice(t, min(MT, t + 3))
                    link(nc.gpsimd.tensor_copy(w_hi[:, a, ts, :], w_raw[:, ts, :]))
                    nc.gpsimd.tensor_tensor(w_lo[:, a, ts, :], w_raw[:, ts, :], w_hi[:, a, ts, :].bitcast(F32), ALU.subtract).then_inc(split_done, 1)
        CONSTS = 10

        @block.scalar
        def _(act):
            def evacuate_hi(ev, dst, src):
                act.wait_ge(misc_full, MISC[ev] + 1)
                nc.scalar.activation(dst, src, ACT.Copy).then_inc(hi_ready, 1)

            for ev in TIMELINE:
                kind = ev[0]
                if kind == "setup_T":
                    act.wait_ge(wT_full, 2)
                    nc.scalar.activation(wqT, ps[:, 0:2, :].rearrange("p a (h d) -> p (a h) d", d=D), ACT.Copy).then_inc(wqT_ready, 1)
                elif kind in ("xT", "post_T"):
                    c = ev[1] if kind == "xT" else CHUNK[ev[1]]
                    evacuate_hi(ev, xT_hi[:, CH * c:CH * c + CH], misc[:])
                elif kind == "kproj":
                    c = ev[1]
                    if c >= 1:
                        act.wait_ge(k_in[c - 1], 16 * 3 * GROUPS)
                    evacuate_hi(ev, k_hi[:], misc[0:GROUPS * LAT, :])
                elif kind == "proj":
                    n = ev[1]
                    if n >= 1:
                        act.wait_ge(q_in[(n - 1) % QRING], 16 * 3 * REP * ((n - 1) // QRING + 1))
                    evacuate_hi(ev, q_hi[:], misc[:])
                elif kind == "exp":
                    _, n, i, j, h = ev
                    p1 = ("p1", *ev[1:])
                    scores = ps[:, BANK[p1], 0:keys_of(p1)]
                    act.wait_ge(nmax_ready, P1[p1] + 1)
                    nc.scalar.activation(scores, scores, ACT.Exp, bias=nmax_h[:, n % 2, i, j, h:h + 1],
                                         accum_out=sums_h[:, n % 2, i, j, h:h + 1]).then_inc(slot_free, 1)
                elif kind == "scale":
                    act.wait_ge(scales_due, SCALED[ev] + 1)
                    nc.scalar.activation(scales[:], scales[:], ACT.Exp).then_inc(scales_ready, 1)
                elif kind == "p2":
                    _, n, kt, p = ev
                    u = SLOT[ev]
                    off = P * max(0, kt - TPC * BLOCKS[n][1])
                    k = PV["pv", n, kt, 0] // 2
                    act.wait_ge(slot_full, u + 1)
                    if k >= KTBUF:
                        act.wait_ge(pv_done, 2 * (k - KTBUF + 1))
                    nc.scalar.activation(probs[:, k % KTBUF, 2 * p:2 * p + 2, off:CH], ps[:, BANK[ev]:BANK[ev] + 2, 0:CH - off], ACT.Exp).then_inc(slot_free, 1)
                elif kind == "post_logits":
                    act.wait_ge(misc_full, MISC[ev] + 1)
                    nc.scalar.activation(enx[:].rearrange("p t e -> p (t e)"), misc[:, 0:TPC * E], ACT.Exp, scale=-1.0).then_inc(logits_read, 1)
                elif kind == "gu":
                    _, m, t = ev
                    k = MT * m + t
                    rows = SI if t == MT - 1 else P
                    act.wait_ge(gu_full, k + 1)
                    if k == 0:
                        act.wait_ge(pv_done, len(PV))
                    nc.scalar.activation(moe[0:rows, k % 2, :], ps[0:rows, 3 * (k % 2), :], ACT.Silu).then_inc(silu_ready, 1)
                elif kind == "fin_copy":
                    m = ev[1]
                    act.wait_ge(down_done, MT * (m + 1))
                    if m >= 1:
                        act.wait_ge(misc_full, MISC["fin_T", m - 1] + 1)
                    nc.scalar.activation(oT, acc[:], ACT.Copy).then_inc(oT_ready, 1)

        @block.vector
        def _(dve):
            links = [0]

            def link(ins):
                links[0] += 1
                ins.then_inc(vec_link, 1)
                dve.wait_ge(vec_link, links[0])

            def moments(src):
                for t in range(TPC):
                    last = nc.vector.bn_stats(stats[:, t, :], src[:, t, :])
                link(last)
                for t in range(TPC):
                    last = nc.vector.bn_aggr(mv[:, t, :], stats[:, t, :])
                last.then_inc(var_ready, 1)

            def normalise(ev, mom, src):
                k = NORMED[ev]
                dve.wait_ge(rstd_ready, LN[mom] + 1)
                if k:
                    before, m = NORMED_ORDER[k - 1]
                    if before == "xn_nrm":
                        dve.wait_ge(misc_full, MISC["xT", m] + 1)
                    elif before == "post_nrm":
                        dve.wait_ge(resid_ready, m + 1)
                    elif before == "post_nrm2":
                        dve.wait_ge(misc_full, MISC["post_T", m] + 1)
                    else:
                        dve.wait_ge(y_ready, m + 1)
                for t in range(TPC):
                    last = nc.vector.tensor_scalar(normed[:, t, :], src[:, t, :], mv[:, t, 0:1], rstd[:, t:t + 1],
                                                   ALU.subtract, ALU.mult)
                return last.then_inc(normed_ready, 1)

            def evacuate_lo(ev, dst, src, hi):
                dve.wait_ge(misc_full, MISC[ev] + 1)
                dve.wait_ge(hi_ready, HILO[ev] + 1)
                nc.vector.tensor_tensor(dst, src, hi.bitcast(F32), ALU.subtract).then_inc(lo_ready, 1)

            def halves(dst_hi, dst_lo, src):
                link(nc.vector.tensor_copy(dst_hi, src))
                return nc.vector.tensor_tensor(dst_lo, src, dst_hi.bitcast(F32), ALU.subtract)

            for ev in TIMELINE:
                kind = ev[0]
                if kind == "xn_mom":
                    c = ev[1]
                    dve.wait_ge(x_in[c], 16)
                    moments(x_sb[:, TPC * c:TPC * c + TPC, :])
                elif kind == "xn_nrm":
                    c = ev[1]
                    normalise(ev, ("xn_mom", c), x_sb[:, TPC * c:TPC * c + TPC, :])
                elif kind == "setup_T":
                    dve.wait_ge(kv_w_in, 32)
                    link(nc.vector.tensor_copy(wkv_hi[:], wkv[:]))
                    nc.vector.tensor_tensor(wkv_lo[:], wkv[:], wkv_hi[:].bitcast(F32), ALU.subtract).then_inc(wkv_ready, 1)
                    dve.wait_ge(wT_full, 1)
                    nc.vector.tensor_copy(smallT[:], ps[:, 2, 0:3 * E]).then_inc(small_ready, 1)
                elif kind == "setup_am":
                    dve.wait_ge(small_ready, 1)
                    link(halves(gwT_hi[:], gwT_lo[:], smallT[:, 2 * E:3 * E]))
                    dve.wait_ge(am_full, 1)
                    link(nc.vector.tensor_scalar(a_s[:], ps[:, 3, 0:HEADS * LAT], SCALE, None, ALU.mult))
                    link(halves(a_hi[:], a_lo[:], a_s[:]))
                    dve.wait_ge(am_full, 2)
                    nc.vector.tensor_copy(m_sb[:].rearrange("p g d -> p (g d)"), ps[:, 4, 0:GROUPS * D]).then_inc(setup_done, 1)
                elif kind == "xT":
                    c = ev[1]
                    evacuate_lo(ev, xT_lo[:, CH * c:CH * c + CH], misc[:], xT_hi[:, CH * c:CH * c + CH])
                elif kind == "kproj":
                    c = ev[1]
                    evacuate_lo(ev, k_lo[:], misc[0:GROUPS * LAT, :], k_hi[:])
                elif kind == "proj":
                    n = ev[1]
                    evacuate_lo(ev, q_lo[:], misc[:], q_hi[:])
                elif kind == "vproj":
                    c = ev[1]
                    dve.wait_ge(misc_full, MISC[ev] + 1)
                    nc.vector.tensor_copy(v_sb[:, TPC * c:TPC * c + TPC, :].rearrange("p t l -> p (t l)"),
                                          misc[:, 0:TPC * GROUPS * LAT]).then_inc(misc_free, 1)
                elif kind == "p1":
                    _, n, i, j, h = ev
                    dve.wait_ge(slot_full, SLOT[ev] + 1)
                    nc.vector.tensor_reduce(nmax_h[:, n % 2, i, j, h:h + 1], ps[:, BANK[ev], 0:keys_of(ev)],
                                            AX.X, ALU.max, negate=True).then_inc(nmax_ready, 1)
                elif kind == "split":
                    n = ev[1]
                    dve.wait_ge(nmax_ready, P1[P1_LAST[n]] + 1)
                    left = nmax_h[:, n % 2, :, :, 0]
                    if BLOCKS[n][1]:
                        link(nc.vector.tensor_tensor(nmax[:], nmax_h[:, n % 2, :, :, 0], nmax_h[:, n % 2, :, :, 1], ALU.min))
                        left = nmax[:]
                        nc.vector.tensor_tensor(scales[:], nmax[:].unsqueeze(3).to_broadcast([P, TPC, REP, CPB]),
                                                nmax_h[:, n % 2], ALU.subtract).then_inc(scales_due, 1)
                    if n >= 1:
                        dve.wait_ge(misc_full, MISC["shift", n - 1] + 1)
                    for part in range(3):
                        ins = nc.vector.tensor_copy(nm3[:, :, part, :], left)
                        if part == 2:
                            ins.then_inc(nm3_ready, 1)
                            break
                        link(ins)
                        link(nc.vector.tensor_tensor(nm_rest[:, part], left, nm3[:, :, part, :], ALU.subtract))
                        left = nm_rest[:, part]
                elif kind == "shift":
                    n = ev[1]
                    dve.wait_ge(misc_full, MISC[ev] + 1)
                    if n >= 2:
                        dve.wait_ge(shift_in[(n - 2) % QRING], 48 * ((n - 2) // QRING + 1))
                    nc.vector.tensor_copy(shift_rows[:, n % 2, :], misc[0:3 * REP, :]).then_inc(shift_ready, 1)
                elif kind == "rs":
                    n = ev[1]
                    dve.wait_ge(slot_free, EXP[P1_LAST[n]] + 1)
                    total = sums_h[:, n % 2, :, :, 0]
                    if BLOCKS[n][1]:
                        dve.wait_ge(scales_ready, SCALED["scale", n] + 1)
                        link(nc.vector.tensor_tensor(scaled[:], sums_h[:, n % 2], scales[:], ALU.mult))
                        link(nc.vector.tensor_tensor(sums[:], scaled[:, :, :, 0], scaled[:, :, :, 1], ALU.add))
                        total = sums[:]
                    link(nc.vector.reciprocal(rsum[:], total))
                    if n >= 1:
                        dve.wait_ge(misc_full, MISC["rb", n - 1] + 1)
                    nc.vector.tensor_copy(rsum_w[:], rsum[:].unsqueeze(3).to_broadcast([P, TPC, REP, LAT])).then_inc(rsum_ready, 1)
                elif kind == "rb":
                    n = ev[1]
                    dve.wait_ge(misc_full, MISC[ev] + 1)
                    if n >= 2:
                        dve.wait_ge(ylat_ready, n - 1)
                    nc.vector.tensor_copy(rb[:, n % 2, :], misc[:]).then_inc(misc_free, 1)
                elif kind == "yl":
                    n = ev[1]
                    b, c, g = BLOCKS[n]
                    dve.wait_ge(pv_done, PV["pv", n, block_kts(n) - 1, 1] + 1)
                    dve.wait_ge(misc_free, FREED["rb", n] + 1)
                    if n >= GROUPS:
                        dve.wait_ge(misc_full, MISC["post_out", n // GROUPS - 1] + 1)
                    nc.vector.tensor_tensor(ylat[:, g, :], acc[:], rb[:, n % 2, :], ALU.mult).then_inc(ylat_ready, 1)
                elif kind == "post_mom":
                    m = ev[1]
                    dve.wait_ge(misc_full, MISC["post_out", m] + 1)
                    moments(misc[:].rearrange("p (t d) -> p t d", d=D))
                elif kind == "post_nrm":
                    m = ev[1]
                    normalise(ev, ("post_mom", m), misc[:].rearrange("p (t d) -> p t d", d=D))
                elif kind == "post_mom2":
                    m = ev[1]
                    dve.wait_ge(resid_ready, m + 1)
                    moments(x_sb[:, TPC * CHUNK[m]:TPC * CHUNK[m] + TPC, :])
                elif kind == "post_nrm2":
                    m = ev[1]
                    normalise(ev, ("post_mom2", m), x_sb[:, TPC * CHUNK[m]:TPC * CHUNK[m] + TPC, :])
                elif kind == "post_T":
                    m = ev[1]
                    cols = slice(CH * CHUNK[m], CH * CHUNK[m] + CH)
                    evacuate_lo(ev, xT_lo[:, cols], misc[:], xT_hi[:, cols])
                elif kind == "route":
                    _, m, step = ev
                    if step == 0:
                        dve.wait_ge(logits_read, m + 1)
                        dve.wait_ge(consts, CONSTS)
                        dve.wait_ge(bias_in, 16)
                        link(nc.vector.tensor_scalar(score[:], enx[:], 1.0, None, ALU.add))
                        link(nc.vector.reciprocal(score[:], score[:]))
                        link(nc.vector.tensor_tensor(biased[:], score[:], bias[:].unsqueeze(1).to_broadcast([P, TPC, E]), ALU.add))
                    elif step == 1:
                        for t in range(TPC):
                            for g in range(EG):
                                last = nc.vector.max(top_g[:, t, g, :], biased[:, t, EPG * g:EPG * g + EPG])
                        link(last)
                        link(nc.vector.tensor_tensor(gscore[:], top_g[:, :, :, 0], top_g[:, :, :, 1], ALU.add))
                    elif step == 2:
                        other = gscore[:].unsqueeze(2).to_broadcast([P, TPC, EG, EG])
                        own = gscore[:].unsqueeze(3).to_broadcast([P, TPC, EG, EG])
                        nc.vector.tensor_tensor(above[:], other, own, ALU.is_gt)
                        link(nc.vector.tensor_tensor(ties[:], other, own, ALU.is_equal))
                        link(nc.vector.tensor_tensor(ties[:], ties[:], lower[:].unsqueeze(1).to_broadcast([P, TPC, EG, EG]), ALU.mult))
                        link(nc.vector.tensor_tensor(above[:], above[:], ties[:], ALU.add))
                        link(nc.vector.tensor_reduce(rank[:], above[:], AX.X, ALU.add))
                        link(nc.vector.tensor_scalar(gtake[:], rank[:], float(GTOP), None, ALU.is_lt))
                    elif step == 3:
                        nc.vector.tensor_scalar(gout[:], gtake[:], 1.0, BIG, ALU.subtract, ALU.mult)
                        link(nc.vector.tensor_tensor(biased[:].rearrange("p t (g e) -> p t g e", e=EPG),
                                                     biased[:].rearrange("p t (g e) -> p t g e", e=EPG),
                                                     gtake[:].unsqueeze(3).to_broadcast([P, TPC, EG, EPG]), ALU.mult))
                        link(nc.vector.tensor_tensor(cand[:, :, 0:E].rearrange("p t (g e) -> p t g e", e=EPG),
                                                     biased[:].rearrange("p t (g e) -> p t g e", e=EPG),
                                                     gout[:].unsqueeze(3).to_broadcast([P, TPC, EG, EPG]), ALU.add))
                    elif step == 4:
                        for t in range(TPC):
                            last = nc.vector.max(top8[:, t, :], cand[:, t, :])
                        link(last)
                    elif step == 5:
                        for t in range(TPC):
                            nc.vector.max_index(top_at[:, t, :], top8[:, t, :], cand[:, t, :])
                            last = nc.vector.match_replace(cand_rep[:, t, :], top8[:, t, :], cand[:, t, :], -SENTINEL)
                        link(last)
                    elif step == 6:
                        link(nc.vector.tensor_tensor(cw[:, 0], cand_rep[:, :, 0:E], cand[:, :, 0:E], ALU.not_equal))
                        link(nc.vector.tensor_tensor(score[:], score[:], cw[:, 0], ALU.mult))
                        link(nc.vector.tensor_reduce(wsum[:], score[:], AX.X, ALU.add))
                        link(nc.vector.tensor_scalar(wsum[:], wsum[:], 1e-20, None, ALU.add))
                        link(nc.vector.reciprocal(wsum[:], wsum[:]))
                        link(nc.vector.scalar_tensor_tensor(cw[:, 0], score[:], ROUTED_SCALE, wsum[:].unsqueeze(2).to_broadcast([P, TPC, E]),
                                                            ALU.mult, ALU.mult))
                    elif step == 7:
                        if m >= 1:
                            dve.wait_ge(misc_full, MISC["post_cwT", m - 1] + 1)
                        for part in range(3):
                            link(nc.vector.tensor_copy(weights[:, :, E * part:E * part + E], cw[:, part % 2]))
                            if part < 2:
                                link(nc.vector.tensor_tensor(cw[:, (part + 1) % 2], cw[:, part % 2],
                                                             weights[:, :, E * part:E * part + E], ALU.subtract))
                    elif step == 8:
                        link(nc.vector.tensor_copy(best[:], top_at[:, :, 2]))
                        link(nc.vector.tensor_tensor(dist[:, 0], best[:].unsqueeze(2).to_broadcast([P, TPC, L]),
                                                     anchor_lo[:].unsqueeze(1).to_broadcast([P, TPC, L]), ALU.subtract))
                        link(nc.vector.tensor_scalar(dist[:, 1], dist[:, 0], 0.0, None, ALU.is_ge))
                        nc.vector.scalar_tensor_tensor(weights[:, :, 3 * E:WROWS], dist[:, 0], float(E // L), dist[:, 1],
                                                       ALU.is_lt, ALU.mult).then_inc(weights_ready, 1)
                elif kind == "post_cwT":
                    m = ev[1]
                    dve.wait_ge(misc_full, MISC[ev] + 1)
                    nc.vector.tensor_copy(cwT[:, m, :], misc_bf[0:WROWS, 0:CH]).then_inc(cwT_ready, 1)
                elif kind == "gu":
                    _, m, t = ev
                    k = MT * m + t
                    rows = SI if t == MT - 1 else P
                    bank = 3 * (k % 2)
                    dve.wait_ge(silu_ready, k + 1)
                    if k >= 2:
                        dve.wait_ge(down_done, k - 1)
                    if t == MT - 1:
                        nc.vector.tensor_tensor(moe[0:rows, 4 + k % 2, :], moe[0:rows, k % 2, :], ps[0:rows, bank + 1, :], ALU.mult).then_inc(h_ready, 1)
                    else:
                        link(nc.vector.tensor_tensor(moe[:, 2 + k % 2, :], moe[:, k % 2, :], ps[:, bank + 1, :], ALU.mult))
                        nc.vector.tensor_tensor(moe[:, 4 + k % 2, :], moe[:, 2 + k % 2, :], ps[:, bank + 2, :], ALU.mult).then_inc(h_ready, 1)
                elif kind == "fin_mom":
                    m = ev[1]
                    dve.wait_ge(misc_full, MISC["fin_T", m] + 1)
                    moments(misc[:].rearrange("p (t d) -> p t d", d=D))
                elif kind == "fin_nrm":
                    m = ev[1]
                    normalise(ev, ("fin_mom", m), misc[:].rearrange("p (t d) -> p t d", d=D))

        @block.tensor
        def _(pe):
            def misc_turn(ev):
                k = MISC[ev]
                if k == 0:
                    return
                before = MISC_ORDER[k - 1]
                if before[0] in ("xT", "kproj", "proj", "post_T"):
                    pe.wait_ge(lo_ready, HILO[before] + 1)
                elif before[0] == "shift":
                    pe.wait_ge(shift_ready, before[1] + 1)
                elif before[0] == "post_logits":
                    pe.wait_ge(logits_read, before[1] + 1)
                elif before[0] == "post_cwT":
                    pe.wait_ge(cwT_ready, before[1] + 1)
                elif before[0] in ("post_out", "fin_T"):
                    pe.wait_ge(normed_ready, NORMED[before[0].replace("out", "nrm").replace("T", "nrm"), before[1]] + 1)
                else:
                    pe.wait_ge(misc_free, FREED[before] + 1)

            def three(dst, lhs, rhs):
                nc.tensor.matmul(dst, lhs[0], rhs[0], start=True, stop=False)
                nc.tensor.matmul(dst, lhs[0], rhs[1], start=False, stop=False)
                return nc.tensor.matmul(dst, lhs[1], rhs[0], start=False, stop=True)

            for ev in TIMELINE:
                kind = ev[0]
                if kind == "setup_T":
                    pe.wait_ge(up_w_in, 16 * 3)
                    for r in range(3):
                        last = nc.tensor.transpose(ps[:, 2, E * r:E * r + E], small[:, r, :], ident[0:E, 0:E])
                    last.then_inc(wT_full, 1)
                    pe.wait_ge(attn_w_in, 16 * 2)
                    for h in range(HEADS):
                        last = nc.tensor.transpose(ps[:, h // 4, D * (h % 4):D * (h % 4) + D], wq_sb[:, HD * h:HD * h + HD], ident[:])
                    last.then_inc(wT_full, 1)
                elif kind == "setup_am":
                    pe.wait_ge(wqT_ready, 1)
                    pe.wait_ge(small_ready, 1)
                    for h in range(HEADS):
                        last = nc.tensor.matmul(ps[:, 3, LAT * h:LAT * h + LAT], wqT[:, h, :], smallT[:, 0:LAT], start=True, stop=True)
                    last.then_inc(am_full, 1)
                    for h in range(HEADS):
                        g, j = h // REP, h % REP
                        last = nc.tensor.matmul(ps[LAT * j:LAT * j + LAT, 4, D * g:D * g + D], smallT[:, E:E + LAT], wo_sb[:, h, :], start=True, stop=True)
                    last.then_inc(am_full, 1)
                elif kind in ("xT", "post_T"):
                    if kind == "xT" and ev[1] == 0:
                        pe.wait_ge(consts, 1)
                    pe.wait_ge(normed_ready, NORMED["xn_nrm" if kind == "xT" else "post_nrm2", ev[1]] + 1)
                    misc_turn(ev)
                    for t in range(TPC):
                        last = nc.tensor.transpose(misc[:, P * t:P * t + P], normed[:, t, :], ident[:])
                    last.then_inc(misc_full, 1)
                elif kind == "kproj":
                    c = ev[1]
                    cols = slice(CH * c, CH * c + CH)
                    misc_turn(ev)
                    if c == 0:
                        pe.wait_ge(wkv_ready, 1)
                    pe.wait_ge(lo_ready, HILO["xT", c] + 1)
                    three(misc[:], (wkv_hi[:], wkv_lo[:]), (xT_hi[:, cols], xT_lo[:, cols])).then_inc(misc_full, 1)
                elif kind == "vproj":
                    c = ev[1]
                    misc_turn(ev)
                    wv = slice(GROUPS * LAT, 2 * GROUPS * LAT)
                    for t in range(TPC):
                        cols = slice(CH * c + P * t, CH * c + P * t + P)
                        last = three(misc[:, GROUPS * LAT * t:GROUPS * LAT * (t + 1)], (xT_hi[:, cols], xT_lo[:, cols]), (wkv_hi[:, wv], wkv_lo[:, wv]))
                    last.then_inc(misc_full, 1)
                elif kind == "proj":
                    n = ev[1]
                    b, c, g = BLOCKS[n]
                    m = CPB * b + c
                    cols = slice(CH * m, CH * m + CH)
                    heads = slice(REP * LAT * g, REP * LAT * (g + 1))
                    misc_turn(ev)
                    if n == 0:
                        pe.wait_ge(setup_done, 1)
                    pe.wait_ge(lo_ready, HILO["xT", m] + 1)
                    three(misc[:], (a_hi[:, heads], a_lo[:, heads]), (xT_hi[:, cols], xT_lo[:, cols])).then_inc(misc_full, 1)
                elif kind == "p1":
                    _, n, i, j, h = ev
                    b, c, g = BLOCKS[n]
                    if (i, j, h) == (0, 0, 0):
                        pe.wait_ge(q_in[n % QRING], 16 * 3 * REP * (n // QRING + 1))
                        for cc in range(c + 1):
                            pe.wait_ge(k_in[CPB * b + cc], 16 * 3 * GROUPS)
                        pe.wait_ge(consts, 6)
                    if EXPS_BEFORE[ev]:
                        pe.wait_ge(slot_free, EXPS_BEFORE[ev])
                    at = T * b + CH * h
                    keys = keys_of(ev)
                    last = nc.tensor.matmul(ps[:, BANK[ev], 0:keys], qst[0:QROWS, n % QRING, j, P * i:P * i + P], kst[0:QROWS, g, at:at + keys],
                                            start=True, stop=(h < c))
                    if h == c:
                        last = nc.tensor.matmul(ps[:, BANK[ev], P * i:P * i + P], ident_bf[:], mask1[:], start=False, stop=True)
                    last.then_inc(slot_full, 1)
                elif kind == "shift":
                    n = ev[1]
                    misc_turn(ev)
                    pe.wait_ge(nm3_ready, n + 1)
                    for i in range(TPC):
                        last = nc.tensor.matmul(misc[0:3 * REP, P * i:P * i + P], nm3[:, i].rearrange("p a j -> p (a j)"), ident_bf[:], start=True, stop=True)
                    last.then_inc(misc_full, 1)
                elif kind == "rb":
                    n = ev[1]
                    misc_turn(ev)
                    pe.wait_ge(rsum_ready, n + 1)
                    for i in range(TPC):
                        last = nc.tensor.transpose(misc[:, P * i:P * i + P], rsum_w[:, i].rearrange("p j l -> p (j l)"), ident[:])
                    last.then_inc(misc_full, 1)
                elif kind == "p2":
                    _, n, kt, p = ev
                    b, c, g = BLOCKS[n]
                    u = SLOT[ev]
                    diag = kt >= TPC * c
                    off = P * max(0, kt - TPC * c)
                    if (kt, p) == (0, 0):
                        pe.wait_ge(shift_in[n % QRING], 48 * (n // QRING + 1))
                    pe.wait_ge(slot_free, EXPS_BEFORE[ev])
                    at = T * b + P * kt
                    for r in range(2):
                        j = 2 * p + r
                        last = nc.tensor.matmul(ps[:, BANK[ev] + r, 0:CH - off], kst[0:KROWS, g, at:at + P], qst[0:KROWS, n % QRING, j, off:CH], start=True, stop=not diag)
                        if diag:
                            last = nc.tensor.matmul(ps[:, BANK[ev] + r, 0:P], ident_bf[:], mask2[:], start=False, stop=True)
                    last.then_inc(slot_full, 1)
                elif kind == "pv":
                    _, n, kt, h = ev
                    b, c, g = BLOCKS[n]
                    k = PV[ev] // 2
                    off = P * max(0, kt - TPC * c)
                    half_cols = (CH - off) // 2
                    cols = slice(off + half_cols * h, off + half_cols * (h + 1))
                    pe.wait_ge(slot_free, EXP["p2", n, kt, 1] + 1)
                    if kt == 0 and h == 0 and n >= 1:
                        pe.wait_ge(ylat_ready, n)
                    if kt == 0:
                        for cc in range(c + 1):
                            pe.wait_ge(misc_free, FREED["vproj", CPB * b + cc] + 1)
                    for j in range(REP):
                        last = nc.tensor.matmul(acc[LAT * j:LAT * j + LAT, cols], v_sb[:, (T // P) * b + kt, LAT * g:LAT * g + LAT], probs[:, k % KTBUF, j, cols],
                                                start=(kt == 0 and h == 0), stop=(kt == block_kts(n) - 1 and h == 1))
                    last.then_inc(pv_done, 1)
                elif kind == "post_out":
                    m = ev[1]
                    misc_turn(ev)
                    pe.wait_ge(ylat_ready, GROUPS * (m + 1))
                    for t in range(TPC):
                        for g in range(GROUPS):
                            last = nc.tensor.matmul(misc[:, D * t:D * t + D], ylat[:, g, P * t:P * t + P], m_sb[:, g, :], start=(g == 0), stop=(g == GROUPS - 1))
                    last.then_inc(misc_full, 1)
                elif kind == "post_logits":
                    m = ev[1]
                    misc_turn(ev)
                    pe.wait_ge(lo_ready, HILO["post_T", m] + 1)
                    for t in range(TPC):
                        cols = slice(CH * CHUNK[m] + P * t, CH * CHUNK[m] + P * t + P)
                        last = three(misc[:, E * t:E * t + E], (xT_hi[:, cols], xT_lo[:, cols]), (gwT_hi[:], gwT_lo[:]))
                    last.then_inc(misc_full, 1)
                elif kind == "post_cwT":
                    m = ev[1]
                    misc_turn(ev)
                    pe.wait_ge(weights_ready, m + 1)
                    for t in range(TPC):
                        last = nc.tensor.transpose(misc_bf[0:WROWS, P * t:P * t + P], weights[:, t, :], ident_bf[:])
                    last.then_inc(misc_full, 1)
                elif kind == "gu":
                    _, m, t = ev
                    k = MT * m + t
                    bank = 3 * (k % 2)
                    cols = slice(CH * CHUNK[m], CH * CHUNK[m] + CH)
                    if k == 0:
                        pe.wait_ge(split_done, 2 * len(WSPLITS))
                        pe.wait_ge(slot_free, len(SLOT))
                    if t == 0:
                        pe.wait_ge(cwT_ready, m + 1)
                        pe.wait_ge(consts, CONSTS)
                    if k >= 2:
                        pe.wait_ge(h_ready, k - 1)
                    for a in range(2):
                        last = three(ps[:, bank + a, :], (w_hi[:, a, t, :], w_lo[:, a, t, :]), (xT_hi[:, cols], xT_lo[:, cols]))
                    if t < MT - 1:
                        last = nc.tensor.matmul(ps[:, bank + 2, :], sel[:, t, :], cwT[:, m, :], start=True, stop=True)
                    last.then_inc(gu_full, 1)
                elif kind == "down":
                    _, m, t = ev
                    k = MT * m + t
                    rows = SI if t == MT - 1 else P
                    pe.wait_ge(h_ready, k + 1)
                    if k == 0:
                        pe.wait_ge(anchors_scaled, 1)
                        pe.wait_ge(ylat_ready, NB)
                    if t == 0 and m >= 1:
                        pe.wait_ge(oT_ready, m)
                    nc.tensor.matmul(acc[:], wd[0:rows, t, :], moe[0:rows, 4 + k % 2, :], start=(t == 0), stop=(t == MT - 1)).then_inc(down_done, 1)
                elif kind == "fin_T":
                    m = ev[1]
                    misc_turn(ev)
                    pe.wait_ge(oT_ready, m + 1)
                    for t in range(TPC):
                        last = nc.tensor.transpose(misc[:, P * t:P * t + P], oT[:, P * t:P * t + P], ident[:])
                    last.then_inc(misc_full, 1)


MISC_ORDER = sorted(MISC, key=MISC.get)
FREED = {ev: k for k, ev in enumerate(e for e in MISC_ORDER if e[0] in ("vproj", "rb"))}
SCALED = {ev: k for k, ev in enumerate(e for e in TIMELINE if e[0] == "scale")}
NORMED_ORDER = [e for e in TIMELINE if e[0] in ("xn_nrm", "post_nrm", "post_nrm2", "fin_nrm")]
NORMED = {ev: k for k, ev in enumerate(NORMED_ORDER)}

_NAMES = ["attn_x", "attn_wq", "attn_wk_down", "attn_wv_down", "attn_wk_up", "attn_wv_up", "attn_wo", "ffn_gate_weight", "ffn_gate_bias",
          "ffn_w_gate", "ffn_w_up", "ffn_w_down", "ffn_shared_w_gate", "ffn_shared_w_up", "ffn_shared_w_down", "ffn_anchor_w_gate",
          "ffn_anchor_w_up", "ffn_anchor_w_down"]


def kernel(**inputs):
    import numpy as np
    import concourse.bacc as bacc
    from concourse.bass_utils import run_bass_kernel_spmd

    nc = bacc.Bacc("TRN2", target_bir_lowering=False, num_devices=1)
    arrays, args = {}, []
    for name in _NAMES:
        a = np.ascontiguousarray(inputs[f"L0_{name}"])
        arrays[f"in_{name}"] = a
        args.append(nc.dram_tensor(f"in_{name}", a.shape, mybir.dt.from_np(a.dtype), kind="ExternalInput").ap())
    args.append(nc.dram_tensor("result", (B, T, D), F32, kind="ExternalOutput").ap())
    build(nc, *args)
    r = run_bass_kernel_spmd(nc, [arrays], core_ids=[0])
    return r.results[0]["result"]
```
